# Optimizing a Trainium2 kernel written in Bass

```python
import numpy as np
import jax
import jax.numpy as jnp

def _softmax(x, axis=-1):
    return jax.nn.softmax(x, axis=axis)

def _gelu(x):
    return jax.nn.gelu(x, approximate=True)

def _silu(x):
    return jax.nn.silu(x)

def _sigmoid(x):
    return jax.nn.sigmoid(x)

def _layernorm(x, axis=-1, eps=1e-05):
    m = jnp.mean(x, axis=axis, keepdims=True)
    v = jnp.var(x, axis=axis, keepdims=True)
    return (x - m) / jnp.sqrt(v + eps)

def _scatter_add(tgt, idx, src, axis=0):
    return tgt.at[idx].add(src)

def _segment_sum(src, seg, n):
    return jax.ops.segment_sum(src, seg, n)
kernel_name = 'mk_vit_tower_cls_d1_tok_img512_r4_693f46'

def setup_inputs(seed: int=0):
    np.random.seed(seed)
    _w = jnp.asarray

    def _rec_inputs():
        import jax
        import jax.numpy as jnp
        _rk = jax.random.key(seed)
        x = -7.10856e-05 + 0.999911 * jax.random.normal(jax.random.fold_in(_rk, 1), (128, 64, 64, 128), jnp.float32)
        cls_tok = 0.02 * jax.random.normal(jax.random.fold_in(_rk, 5), (1, 1, 128), jnp.float32)
        return (x, cls_tok)
    x, cls_tok = _rec_inputs()

    def _L0_tok_setup():
        import jax, jax.numpy as jnp
        import numpy as np
        from jax import lax
        B, H, W, C = (32, 64, 64, 128)
        POOL = 8
        STRIDE = 8
        key = jax.random.key(seed)
        k1, k2, k3 = jax.random.split(key, 3)
        x = jax.random.normal(k1, (B, H, W, C), dtype=jnp.float32)
        conv_w = jax.random.normal(k2, (3, 3, 1, C), dtype=jnp.float32) * 0.02
        conv_b = jax.random.normal(k3, (C,), dtype=jnp.float32) * 0.02
        return {'x': x, 'conv_w': conv_w, 'conv_b': conv_b}
    _L0_tok_all = _L0_tok_setup()
    _L0_tok_in = {k: v for k, v in _L0_tok_all.items() if k in ('conv_w', 'conv_b')}
    del _L0_tok_all

    def _L0_attn_setup():
        import jax, jax.numpy as jnp
        import numpy as np
        STAGES = 3
        CAUSAL = True

        def _positional_encoding(T, W):
            half = W // 2
            t = jnp.arange(T, dtype=jnp.float32)
            freqs = 10000.0 ** (-jnp.arange(half, dtype=jnp.float32) / half)
            phi = t[:, None] * freqs[None, :]
            return jnp.concatenate([jnp.sin(phi), jnp.cos(phi)], axis=-1)
        key = jax.random.key(seed)
        k1, k2, k3 = jax.random.split(key, 3)
        B, T, W = (4, 512, 128)
        X = jax.random.normal(k1, (B, T, W), dtype=jnp.float32)
        W_proj = jax.random.normal(k2, (W, W, STAGES + 1), dtype=jnp.float32) * 0.02
        W_filt = jax.random.normal(k3, (W, W, STAGES), dtype=jnp.float32) * 0.02
        return {'X': X, 'W_proj': W_proj, 'W_filt': W_filt}
    _L0_attn_all = _L0_attn_setup()
    _L0_attn_in = {k: v for k, v in _L0_attn_all.items() if k in ('W_proj', 'W_filt')}
    del _L0_attn_all

    def _L0_ffn_setup():
        import jax, jax.numpy as jnp
        import numpy as np
        EPS = 1e-05
        TOP_K = 2

        def layer_norm(x, g, b):
            m = x.mean(-1, keepdims=True)
            v = ((x - m) ** 2).mean(-1, keepdims=True)
            return (x - m) / jnp.sqrt(v + EPS) * g + b
        key = jax.random.key(seed)
        ks = jax.random.split(key, 8)
        B, S, D, E, H = (8, 128, 128, 8, 512)
        x = jax.random.normal(ks[0], (B, S, D), dtype=jnp.float32)
        Wg = jax.random.normal(ks[1], (D, E), dtype=jnp.float32) * 0.02
        W1 = jax.random.normal(ks[2], (E, D, H), dtype=jnp.float32) * 0.02
        b1 = jnp.zeros((E, H), dtype=jnp.float32)
        W2 = jax.random.normal(ks[3], (E, H, D), dtype=jnp.float32) * 0.02
        b2 = jnp.zeros((E, D), dtype=jnp.float32)
        ln_g = jnp.ones((D,), dtype=jnp.float32)
        ln_b = jnp.zeros((D,), dtype=jnp.float32)
        out_g = jnp.ones((D,), dtype=jnp.float32)
        out_b = jnp.zeros((D,), dtype=jnp.float32)
        return {'x': x, 'Wg': Wg, 'W1': W1, 'b1': b1, 'W2': W2, 'b2': b2, 'ln_g': ln_g, 'ln_b': ln_b, 'out_g': out_g, 'out_b': out_b}
    _L0_ffn_all = _L0_ffn_setup()
    _L0_ffn_in = {k: v for k, v in _L0_ffn_all.items() if k in ('Wg', 'W1', 'b1', 'W2', 'b2', 'ln_g', 'ln_b', 'out_g', 'out_b')}
    del _L0_ffn_all
    return {'x': x, 'cls_tok': cls_tok, 'L0_tok_conv_w': _L0_tok_in['conv_w'], 'L0_tok_conv_b': _L0_tok_in['conv_b'], 'L0_attn_W_proj': _L0_attn_in['W_proj'], 'L0_attn_W_filt': _L0_attn_in['W_filt'], 'L0_ffn_Wg': _L0_ffn_in['Wg'], 'L0_ffn_W1': _L0_ffn_in['W1'], 'L0_ffn_b1': _L0_ffn_in['b1'], 'L0_ffn_W2': _L0_ffn_in['W2'], 'L0_ffn_b2': _L0_ffn_in['b2'], 'L0_ffn_ln_g': _L0_ffn_in['ln_g'], 'L0_ffn_ln_b': _L0_ffn_in['ln_b'], 'L0_ffn_out_g': _L0_ffn_in['out_g'], 'L0_ffn_out_b': _L0_ffn_in['out_b']}

def reference(x, cls_tok, L0_tok_conv_w, L0_tok_conv_b, L0_attn_W_proj, L0_attn_W_filt, L0_ffn_Wg, L0_ffn_W1, L0_ffn_b1, L0_ffn_W2, L0_ffn_b2, L0_ffn_ln_g, L0_ffn_ln_b, L0_ffn_out_g, L0_ffn_out_b):
    import jax
    import jax.numpy as jnp

    def _L0_tok_ref(x, conv_w, conv_b):
        import jax, jax.numpy as jnp
        import numpy as np
        from jax import lax
        B, H, W, C = (32, 64, 64, 128)
        POOL = 8
        STRIDE = 8
        y = lax.conv_general_dilated(x, conv_w, window_strides=(1, 1), padding=[(1, 1), (1, 1)], dimension_numbers=('NHWC', 'HWIO', 'NHWC'), feature_group_count=C) + conv_b
        y = lax.reduce_window(y, jnp.float32(0.0), lax.add, (1, POOL, POOL, 1), (1, STRIDE, STRIDE, 1), 'VALID') / jnp.float32(POOL * POOL)
        b = y.shape[0]
        ct = y.reshape(b, -1, C)
        return ct

    def _L0_attn_ref(X, W_proj, W_filt):
        import jax, jax.numpy as jnp
        import numpy as np
        STAGES = 3
        CAUSAL = True

        def _positional_encoding(T, W):
            half = W // 2
            t = jnp.arange(T, dtype=jnp.float32)
            freqs = 10000.0 ** (-jnp.arange(half, dtype=jnp.float32) / half)
            phi = t[:, None] * freqs[None, :]
            return jnp.concatenate([jnp.sin(phi), jnp.cos(phi)], axis=-1)
        B, T, W = X.shape
        x = jnp.einsum('btw,wvs->btvs', X, W_proj)
        pe = _positional_encoding(T, W)
        f = jnp.einsum('tw,wvs->tvs', pe, W_filt)
        if CAUSAL:
            x = jnp.concatenate([x, jnp.zeros_like(x)], axis=1)
            f = jnp.concatenate([f, jnp.zeros_like(f)], axis=0)
        n = x.shape[1]
        Ff = jnp.fft.rfft(f, axis=0)
        y = x[..., 0]
        for i in range(STAGES):
            Fy = jnp.fft.rfft(y, axis=1)
            y = jnp.fft.irfft(Fy * Ff[None, :, :, i], n=n, axis=1) * x[..., i + 1]
        if CAUSAL:
            y = y[:, :T]
        return y

    def _L0_ffn_ref(x, Wg, W1, b1, W2, b2, ln_g, ln_b, out_g, out_b):
        import jax, jax.numpy as jnp
        import numpy as np
        EPS = 1e-05
        TOP_K = 2

        def layer_norm(x, g, b):
            m = x.mean(-1, keepdims=True)
            v = ((x - m) ** 2).mean(-1, keepdims=True)
            return (x - m) / jnp.sqrt(v + EPS) * g + b
        xn = layer_norm(x, ln_g, ln_b)
        logits = jnp.einsum('bsd,de->bse', xn, Wg)
        probs = jax.nn.softmax(logits, axis=-1)
        top_p, top_i = jax.lax.top_k(probs, TOP_K)
        conf = top_p / top_p.sum(-1, keepdims=True)
        h = jax.nn.gelu(jnp.einsum('bsd,edh->bseh', xn, W1) + b1)
        o = jnp.einsum('bseh,ehd->bsed', h, W2) + b2
        sel = jnp.take_along_axis(o, top_i[..., None], axis=2)
        combined = jnp.einsum('bskd,bsk->bsd', sel, conf)
        return layer_norm(x + combined, out_g, out_b)
    h = _L0_tok_ref(x, L0_tok_conv_w, L0_tok_conv_b)
    h = jnp.concatenate([jnp.broadcast_to(cls_tok, (h.shape[0], 1, h.shape[2])), h], axis=1)
    h = h + _L0_attn_ref(_layernorm(h, axis=-1), L0_attn_W_proj, L0_attn_W_filt)
    h = h + _L0_ffn_ref(_layernorm(h, axis=-1), L0_ffn_Wg, L0_ffn_W1, L0_ffn_b1, L0_ffn_W2, L0_ffn_b2, L0_ffn_ln_g, L0_ffn_ln_b, L0_ffn_out_g, L0_ffn_out_b)
    return h

_drawn_inputs = setup_inputs


def setup_inputs(seed=0):
    import zlib

    import numpy as np

    out = dict(_drawn_inputs(seed))
    spreads = {'L0_ffn_b1': (0.0, 0.488),
     'L0_ffn_b2': (0.0, 0.1),
     'L0_ffn_ln_g': (1.0, 0.2),
     'L0_ffn_ln_b': (0.0, 0.1),
     'L0_ffn_out_g': (1.0, 0.2),
     'L0_ffn_out_b': (0.0, 0.1)}
    factors = {}
    for name, (base, spread) in spreads.items():
        noise = np.random.default_rng([zlib.crc32(name.encode()), seed]).standard_normal(out[name].shape)
        drawn = base * np.exp(spread * noise) if base else spread * noise
        out[name] = jnp.asarray(drawn.astype(out[name].dtype))
    for name, factor in factors.items():
        out[name] = (out[name] * factor).astype(out[name].dtype)
    return out
```

```python
from contextlib import ExitStack

import numpy as np
import concourse.bass as bass
from concourse import mybir

P = 128
B, HW, CH = 128, 64, 128
POOL = 8
NWIN = HW // POOL
T = NWIN * NWIN
STAGES = 3
NE, HID, TOPK = 8, 512, 2
NHC = HID // P
IMG = P // T
TG = 4
NG = B // (IMG * TG)
N = TG * P
NFFT = 2 * T
EPS = 1e-5
ROW = POOL * CH
W9 = NWIN + 1
GRID = IMG * TG * NWIN * W9
PAD = 2
NST = 9
NQ = 16

F32 = mybir.dt.float32
U32 = mybir.dt.uint32
ALU = mybir.AluOpType
ACT = mybir.ActivationFunctionType

ROW_SLOT = {0: 0, 1: 1, 2: 2, 3: 3, 7: 4, 4: 5, 5: 6, 6: 7}
STAT_ROW = (0, 2, 4)
STAT_COL = (0, 1, 7)
TAPS = ((2, -1), (0, 0), (1, 0), (2, 0), (0, 1))


def shape_constants():
    half = CH // 2
    freqs = (10000.0 ** (-np.arange(half, dtype=np.float32) / half)).astype(np.float32)
    phi = np.arange(T + 1, dtype=np.float32)[:, None] * freqs[None, :]
    pe = np.concatenate([np.sin(phi), np.cos(phi)], axis=-1).astype(np.float64)
    theta = 2 * np.pi * np.outer(np.arange(NFFT), np.arange(T)) / NFFT
    cos, sin = np.cos(theta), np.sin(theta)
    dft = np.stack([np.concatenate([cos.T, sin.T], 0), np.concatenate([-sin.T, cos.T], 0)], 1)
    back_re = np.concatenate([cos, sin], 1) / NFFT
    back_im = np.concatenate([-sin, cos], 1) / NFFT
    idft = np.stack([back_re, -back_re, back_im], 1)
    pe_mats = np.stack([pe[:T].T @ cos.T, -(pe[:T].T @ sin.T),
                        np.concatenate([pe[1:T + 1].T] * IMG, 1),
                        np.repeat(pe[0][:, None], P, 1)], 1)
    return {
        "ident": np.eye(P, dtype=np.float32),
        "dft": dft.reshape(P, -1).astype(np.float32),
        "idft": idft.reshape(P, -1).astype(np.float32),
        "pe_mats": pe_mats.reshape(P, -1).astype(np.float32),
        "iota": np.tile(np.arange(NE, dtype=np.float32), (P, 1)),
    }


def build(nc, x, cls_tok, conv_w, conv_b, w_proj, w_filt, w_gate, w1, b1, w2, b2_blocks,
          ln_g, ln_b, out_g, out_b, ident_d, dft_d, idft_d, pe_mats_d, iota_d, out):
    ctx = ExitStack()
    with ctx:
        def sb(name, shape, dt=F32):
            return ctx.enter_context(nc.sbuf_tensor(name, shape, dt))

        def sem(name):
            return ctx.enter_context(nc.semaphore(name))

        def wait(eng, s, value):
            if not isinstance(value, int) or value > 0:
                eng.wait_ge(s, value)

        ident = sb("ident", [P, P])
        dft = sb("dft_sb", [P, 2, P])
        idft = sb("idft_sb", [P, 3, P])
        pe_mats = sb("pe_sb", [P, 4, P])
        iota = sb("iota_sb", [P, NE])
        wf = sb("wf", [P, STAGES * CH])
        wp = sb("wp", [P, (STAGES + 1) * CH])
        wg = sb("wg", [P, NE])
        w1s = sb("w1s", [P, NE, HID])
        w2s = sb("w2s", [P, NE, NHC, CH])
        b1s = sb("b1s", [P, NE, NHC])
        b2s = sb("b2s", [TG * NE, TG, CH])
        ln_gc = sb("ln_gc", [P, 1])
        ln_bc = sb("ln_bc", [P, 1])
        out_gr = sb("out_gr", [P, CH])
        out_br = sb("out_br", [P, CH])
        cw = sb("cw", [P, 3, 3])
        cb = sb("cb", [P, 1])
        coef_r = sb("coef_r", [P, 5, 3])
        coef = sb("coef", [P, 5, 5])
        filt_re = sb("filt_re", [P, STAGES, CH])
        filt_im = sb("filt_im", [P, STAGES, CH])
        cls_part = sb("cls_part", [P, STAGES, CH])

        xb = sb("xb", [P, 2, POOL, ROW])
        stat = sb("stat", [P, NST, PAD + GRID + W9 + 1])
        pooled = sb("pooled", [P, GRID])
        pooledT = sb("pooledT", [P, N])
        h0 = sb("h0", [P, TG, CH])
        hn = sb("hn", [P, TG, CH])
        hnT = sb("hnT", [P, N])
        xp = sb("xp", [P, TG, STAGES + 1, CH])
        prod = sb("prod", [P, 4, TG, CH])
        conv_sum = sb("conv_sum", [P, TG, CH])
        h1 = sb("h1", [P, 2, TG, CH])
        acc = sb("acc", [P, 2, TG, CH])
        xhat = sb("xhat", [P, TG, CH])
        xnT = sb("xnT", [P, 2, N])
        lg = sb("lg", [P, TG, NE])
        top = sb("top", [P, TG, 8])
        top_i = sb("top_i", [P, TG, 8], U32)
        top_f = sb("top_f", [P, TG, 8])
        delta = sb("delta", [P, TG])
        th = sb("th", [P, TG])
        c12 = sb("c12", [P, 2, TG])
        eq = sb("eq", [P, 2, TG, NE])
        conf = sb("conf", [P, 2, TG, NE])
        confT = sb("confT", [TG * NE, P])
        hid = sb("hid", [P, 2, NHC, N])
        ot = sb("ot", [P, TG, CH])
        neg_half = sb("neg_half", [P, TG])
        wait_carrier = sb("wait_carrier", [P, 1])
        eps_t = sb("eps_t", [P, TG])
        bn6 = sb("bn6", [P, TG, 6])
        mv = sb("mv", [P, TG, 2])
        rstd = sb("rstd", [P, TG])
        bn6o = sb("bn6o", [P, TG, 6])
        mvo = sb("mvo", [P, TG, 2])
        rstdo = sb("rstdo", [P, TG])

        bank = [ctx.enter_context(nc.psum_tensor(f"bank{i}", [P, N], F32)) for i in range(8)]
        FFN1_BANK, FFN2_BANK, STAT_BANK, TOK_BANK = (0, 1), 2, (3, 4), (5, 6, 7)

        names = """early_loaded weights_loaded pads_zeroed coef_steps
            sum_steps stat_transposed stat_copied conv_steps
            pooled_transposed h0_ready norm_steps hn_ready hn_transposed hnT_ready
            projected proj_copied spectrum_ready product_ready filtered conv_summed y_ready
            h1_ready base_normed xhat_ready xhat_transposed xnT_ready logits_ready
            gate_steps delta_ready tanh_ready mask_steps conf_ready conf_transposed confT_ready
            bias_ready base_ready ffn1_done gelu_done ffn2_done ffn_added
            out_norm_steps out_normed out_scaled out_summed out_stored
            cls_steps cls_ffn1 cls_gelu cls_ffn2 cls_added cls_out_steps""".split()
        S = {n: sem(n) for n in names}
        x_loaded = [sem("x_loaded0"), sem("x_loaded1")]
        XLOAD = 16 * POOL
        SUMS, CONVS, NORMS = 6, 25, 12
        CLS_OUT = 8

        cls_order = ["normed", "transposed", "hnT", "projected", "xp", "spectra", "spectra_sb"]
        cls_order += [f"{n}{k}" for k in range(STAGES) for n in ("part", "convolved", "y")]
        cls_order += ["h1", "base", "xhat", "xhat_t", "xnT", "logits", "lg", "top", "top_i", "top_f",
                      "delta", "tanh", "c12", "eq", "masked", "conf", "conf_t", "confT", "bias", "base_b"]
        CLS = {n: k + 1 for k, n in enumerate(["n1", "n2", "n3", "n4"] + cls_order[:17]
                                              + ["m1", "m2", "m3", "m4"] + cls_order[17:18]
                                              + ["o1", "o2", "o3", "o4"] + cls_order[18:])}

        block = ctx.enter_context(nc.Block())

        def schedule(eng, step, Fori):
            step(0, 0, True, False, False, False)
            step(1, 1, True, True, False, False)
            step(2, 0, True, True, True, False)
            step(3, 1, True, True, True, True)
            with Fori(2, NG // 2) as pair:
                step(pair * 2, 0, True, True, True, True)
                step(pair * 2 + 1, 1, True, True, True, True)
            step(NG, 0, False, True, True, True)
            step(NG + 1, 1, False, False, True, True)
            step(NG + 2, 0, False, False, False, True)

        @block.sync
        def _(eng):
            early = [(h0[:, 0, :], cls_tok[0, 0, :].partition_broadcast(P)),
                     (ident[:, :], ident_d), (wp[:, :], w_proj), (wf[:, :], w_filt),
                     (pe_mats[:, :, :], pe_mats_d.rearrange("p (a b) -> p a b", a=4)),
                     (wg[:, :], w_gate), (iota[:, :], iota_d), (cw[:, :, :], conv_w), (cb[:, :], conv_b),
                     (ln_gc[:, :], ln_g), (ln_bc[:, :], ln_b),
                     (b2s[:, :, :], b2_blocks)]
            late = [(dft[:, :, :], dft_d.rearrange("p (a b) -> p a b", a=2)),
                    (idft[:, :, :], idft_d.rearrange("p (a b) -> p a b", a=3)),
                    (b1s[:, :, :], b1),
                    (out_gr[:, :], out_g.partition_broadcast(P)), (out_br[:, :], out_b.partition_broadcast(P)),
                    (w1s[:, :, :], w1), (w2s[:, :, :, :], w2)]
            for dst, src in early:
                eng.dma_start(dst, src).then_inc(S["early_loaded"], 16)

            def load_tile(g, t):
                wait(eng, S["stat_transposed"], 12 * g + 3 * t - 3)
                rows = x[bass.ds(g * (IMG * TG) + IMG * t, IMG)].rearrange(
                    "b (i r) (j w) c -> (b i) j r (w c)", r=POOL, w=POOL)
                for r, slot in ROW_SLOT.items():
                    eng.dma_start(xb[:, t % 2, slot, :], rows[:, :, r, :]).then_inc(x_loaded[t % 2], 16)

            def store(g):
                eng.wait_ge(S["out_summed"], g + 1)
                rows = out[bass.ds(g * (IMG * TG), IMG * TG), 1:T + 1, :].rearrange(
                    "(t m) s c -> m s t c", m=IMG)
                for m in range(IMG):
                    eng.dma_start(rows[m], ot[m * T:(m + 1) * T, :, :]).then_inc(S["out_stored"], 16)

            def step(i, par, pool, mix, experts, finish):
                for t in range(TG):
                    if pool:
                        load_tile(i, t)
                    if t == 0 and isinstance(i, int) and i == 0:
                        for dst, src in late:
                            eng.dma_start(dst, src).then_inc(S["weights_loaded"], 16)
                    if t == 0 and isinstance(i, int) and i == 1:
                        eng.wait_ge(S["cls_out_steps"], CLS_OUT)
                        eng.dma_start(out[:, 0, :], ot[:, 0, :]).then_inc(S["cls_out_steps"], 16)
                    if t == 2 and finish:
                        store(i - 3)

            schedule(eng, step, eng.Fori)
            eng.wait_ge(S["cls_out_steps"], CLS_OUT + 16)
            eng.wait_ge(S["out_stored"], 16 * IMG * NG)

        N_EARLY, N_LATE = 16 * 12, 16 * 7

        @block.gpsimd
        def _(eng):
            eng.memset(neg_half[:, :], -0.5).then_inc(S["pads_zeroed"], 1)
            eng.memset(eps_t[:, :], EPS).then_inc(S["pads_zeroed"], 1)
            eng.memset(stat[:, :, :], 0.0).then_inc(S["pads_zeroed"], 1)
            eng.wait_ge(S["pads_zeroed"], 3)

            def affine(o, h, nt, ready, ready_value, scaled, scaled_value, summed):
                eng.wait_ge(ready, ready_value)
                eng.tensor_tensor(o, o, out_gr[:, :].unsqueeze(1).to_broadcast([P, nt, CH]), ALU.mult)\
                   .then_inc(scaled, 1)
                eng.wait_ge(scaled, scaled_value)
                eng.tensor_tensor(o, o, out_br[:, :].unsqueeze(1).to_broadcast([P, nt, CH]), ALU.add)\
                   .then_inc(scaled, 1)
                eng.wait_ge(scaled, scaled_value + 1)
                eng.tensor_tensor(o, o, h, ALU.add).then_inc(summed, 1)

            def inverse_std(s, base, nt, mv, rstd):
                eng.wait_ge(s, base + 2)
                eng.tensor_tensor(rstd[:, 0:nt], mv[:, 0:nt, 1], eps_t[:, 0:nt], ALU.add).then_inc(s, 1)
                eng.wait_ge(s, base + 3)
                eng.tensor_tensor(rstd[:, 0:nt], rstd[:, 0:nt], neg_half[:, 0:nt], ALU.pow).then_inc(s, 1)

            def step(i, par, pool, mix, experts, finish):
                if isinstance(i, int) and i == 1:
                    inverse_std(S["cls_out_steps"], 0, 1, mvo, rstdo)
                    affine(ot[:, 0:1, :], h1[:, 0, 0:1, :], 1, S["cls_out_steps"], 5,
                           S["cls_out_steps"], 6, S["cls_out_steps"])
                if mix:
                    inverse_std(S["norm_steps"], (i - 1) * NORMS, TG, mv, rstd)
                if finish:
                    g = i - 3
                    inverse_std(S["out_norm_steps"], g * 4, TG, mvo, rstdo)
                    affine(ot[:, :, :], h1[:, 1 - par, :, :], TG, S["out_normed"], g + 1,
                           S["out_scaled"], g * 2 + 1, S["out_summed"])
                if mix:
                    for n in (4, 8):
                        inverse_std(S["norm_steps"], (i - 1) * NORMS + n, TG, mv, rstd)

            for v in (0, CLS["h1"], CLS["base"]):
                inverse_std(S["cls_steps"], v, 1, mv, rstd)
            eng.wait_ge(S["weights_loaded"], N_LATE)
            schedule(eng, step, eng.Fori)

        @block.tensor
        def _(eng):
            def mm(o, lhsT, rhs, start=True, stop=True):
                return nc.tensor.matmul(o, lhsT, rhs, start=start, stop=stop)

            def transpose_tiles(o, src, nt):
                for t in range(nt):
                    last = nc.tensor.transpose(o[:, t * P:(t + 1) * P], src(t), ident[:, :])
                return last

            def gate(o, par, nt):
                for t in range(nt):
                    last = mm(o[:, t * NE:(t + 1) * NE], xnT[:, par, t * P:(t + 1) * P], wg[:, :])
                return last

            def cls_chain():
                A, C, D = (bank[b] for b in TOK_BANK)
                s = S["cls_steps"]
                eng.wait_ge(S["early_loaded"], N_EARLY)
                eng.wait_ge(s, CLS["normed"])
                nc.tensor.transpose(C[:, 0:P], hn[:, 0, :], ident[:, :]).then_inc(s, 1)
                eng.wait_ge(s, CLS["hnT"])
                mm(A[:, :], hnT[:, 0:P], wp[:, :]).then_inc(s, 1)
                eng.wait_ge(s, CLS["xp"])
                for n in range(4):
                    last = mm(bank[n][:, 0:STAGES * CH], pe_mats[:, n, :], wf[:, :])
                last.then_inc(s, 1)
                eng.wait_ge(s, CLS["xhat"])
                nc.tensor.transpose(A[:, 0:P], xhat[:, 0, :], ident[:, :]).then_inc(s, 1)
                eng.wait_ge(s, CLS["xnT"])
                gate(C, 0, 1).then_inc(s, 1)
                eng.wait_ge(s, CLS["conf"])
                nc.tensor.transpose(C[0:TG * NE, 0:P], conf[:, 0, :, :].rearrange("p t e -> p (t e)"),
                                    ident[:, :]).then_inc(s, 1)
                eng.wait_ge(s, CLS["confT"])
                mm(D[:, 0:P], confT[0:NE, :], b2s[0:NE, 0, :]).then_inc(s, 1)

            def cls_expert(e, second):
                if not second:
                    if e == 0:
                        eng.wait_ge(S["weights_loaded"], N_LATE)
                    wait(eng, S["cls_gelu"], 4 * (e - 1))
                    for hc in range(NHC):
                        last = mm(bank[FFN1_BANK[e % 2]][:, hc * P:(hc + 1) * P],
                                  w1s[:, e, hc * P:(hc + 1) * P], xnT[:, 0, 0:P])
                    last.then_inc(S["cls_ffn1"], 1)
                else:
                    eng.wait_ge(S["cls_gelu"], 4 * e + 4)
                    wait(eng, S["cls_added"], e)
                    for hc in range(NHC):
                        last = mm(bank[FFN2_BANK][:, 0:CH], hid[:, e % 2, hc, 0:P], w2s[:, e, hc, :],
                                  hc == 0, hc == NHC - 1)
                    last.then_inc(S["cls_ffn2"], 1)

            def stats(g, t, lo, hi):
                if lo == 0:
                    eng.wait_ge(S["sum_steps"], g * (SUMS * TG) + SUMS * (t + 1))
                for j in range(lo, hi):
                    wait(eng, S["stat_copied"], g * 12 + 3 * t + j - 1)
                    for k in range(3):
                        a = STAT_COL[k] * CH
                        last = nc.tensor.transpose(bank[STAT_BANK[(3 * t + j) % 2]][:, k * P:(k + 1) * P],
                                                   xb[:, t % 2, STAT_ROW[j], a:a + CH], ident[:, :])
                    last.then_inc(S["stat_transposed"], 1)

            def ffn1(g, par, e):
                for hc in range(NHC):
                    wait(eng, S["gelu_done"], g * 32 + 4 * e + hc - 1)
                    mm(bank[FFN1_BANK[hc % 2]][:, :], w1s[:, e, hc * P:(hc + 1) * P], xnT[:, par, :])\
                        .then_inc(S["ffn1_done"], 1)

            def ffn2(g, e):
                eng.wait_ge(S["gelu_done"], g * 32 + 4 * e + 4)
                wait(eng, S["ffn_added"], g * 8 + e)
                for t in range(TG):
                    for hc in range(NHC):
                        last = mm(bank[FFN2_BANK][:, t * CH:(t + 1) * CH], hid[:, e % 2, hc, t * P:(t + 1) * P],
                                  w2s[:, e, hc, :], hc == 0, hc == NHC - 1)
                last.then_inc(S["ffn2_done"], 1)

            def mix(g, par, q):
                A, C, D = (bank[b] for b in TOK_BANK)
                if q == 0:
                    eng.wait_ge(S["conv_steps"], g * CONVS + CONVS)
                    wait(eng, S["xnT_ready"], g)
                    for t in range(TG):
                        src = pooledT[:, t * P:(t + 1) * P]
                        last = nc.tensor.transpose(A[:, t * P:(t + 1) * P], src, ident[:, :])
                    last.then_inc(S["pooled_transposed"], 1)
                if q == 1:
                    eng.wait_ge(S["hn_ready"], g + 1)
                    wait(eng, S["confT_ready"], g)
                    transpose_tiles(C, lambda t: hn[:, t, :], TG).then_inc(S["hn_transposed"], 1)
                if q == 2:
                    eng.wait_ge(S["hnT_ready"], g + 1)
                    wait(eng, S["base_ready"], g)
                    for t in range(3):
                        mm(bank[TOK_BANK[t]][:, :], hnT[:, t * P:(t + 1) * P], wp[:, :])\
                            .then_inc(S["projected"], 1)
                if q == 3:
                    eng.wait_ge(S["proj_copied"], g * 4 + 1)
                    mm(A[:, :], hnT[:, 3 * P:4 * P], wp[:, :]).then_inc(S["projected"], 1)
                if q in (4, 6, 8):
                    k = (q - 4) // 2
                    if k == 0:
                        eng.wait_ge(S["proj_copied"], g * 4 + 4)
                    else:
                        eng.wait_ge(S["y_ready"], g * 3 + k)
                    mm(A[:, :], dft[:, 0, :], xp[:, :, k, :])
                    mm(C[:, :], dft[:, 1, :], xp[:, :, k, :]).then_inc(S["spectrum_ready"], 1)
                if q in (5, 7, 9):
                    k = (q - 5) // 2
                    for n, m in enumerate((0, 1, 2, 2)):
                        eng.wait_ge(S["product_ready"], g * 12 + 4 * k + n + 1)
                        last = mm(D[:, :], idft[:, m, :], prod[:, n, :, :], n == 0, n == 3)
                    last.then_inc(S["filtered"], 1)
                if q == 10:
                    eng.wait_ge(S["xhat_ready"], g + 1)
                    transpose_tiles(A, lambda t: xhat[:, t, :], TG).then_inc(S["xhat_transposed"], 1)
                if q == 11:
                    eng.wait_ge(S["xnT_ready"], g + 1)
                    gate(C, par, TG).then_inc(S["logits_ready"], 1)
                if q == 13:
                    eng.wait_ge(S["conf_ready"], g + 1)
                    nc.tensor.transpose(C[0:TG * NE, 0:P], conf[:, par, :, :].rearrange("p t e -> p (t e)"),
                                        ident[:, :]).then_inc(S["conf_transposed"], 1)
                if q == 14:
                    eng.wait_ge(S["confT_ready"], g + 1)
                    mm(D[:, :], confT[:, :], b2s[:, :, :]).then_inc(S["bias_ready"], 1)

            def step(i, par, pool, do_mix, experts, finish):
                first = isinstance(i, int) and i == 0
                for q in range(NQ):
                    if do_mix:
                        mix(i - 1, 1 - par, q)
                    if pool and q in (3, 6, 9, 12):
                        stats(i, q // 3 - 1, 0, 3)
                    if first:
                        cls_expert(q // 2, q % 2)
                    if q % 2 == 0 and experts:
                        ffn1(i - 2, par, q // 2)
                    if q == 1 and finish:
                        ffn2(i - 3, NE - 1)
                    if q % 2 and q > 1 and experts:
                        ffn2(i - 2, q // 2 - 1)

            cls_chain()
            schedule(eng, step, eng.Fori)

        @block.scalar
        def _(eng):
            def act(o, i, f=ACT.Copy, **kw):
                return nc.scalar.activation(o, i, f, **kw)

            def cls_chain():
                A, C, D = (bank[b] for b in TOK_BANK)
                s = S["cls_steps"]
                eng.wait_ge(S["early_loaded"], N_EARLY)
                eng.wait_ge(s, CLS["transposed"])
                act(hnT[:, 0:P], C[:, 0:P]).then_inc(s, 1)
                eng.wait_ge(s, CLS["projected"])
                act(xp[:, 0, :, :].rearrange("p s c -> p (s c)"), A[:, :]).then_inc(s, 1)
                eng.wait_ge(s, CLS["spectra"])
                act(filt_re[:, :, :].rearrange("p s c -> p (s c)"), bank[0][:, 0:STAGES * CH])
                act(filt_im[:, :, :].rearrange("p s c -> p (s c)"), bank[1][:, 0:STAGES * CH]).then_inc(s, 1)
                eng.wait_ge(s, CLS["xhat_t"])
                act(xnT[:, 0, 0:P], A[:, 0:P], ACT.Identity, scale=ln_gc[:, :], bias=ln_bc[:, :]).then_inc(s, 1)
                eng.wait_ge(s, CLS["delta"])
                act(th[:, 0:1], delta[:, 0:1], ACT.Tanh, scale=0.5).then_inc(s, 1)
                eng.wait_ge(s, CLS["conf_t"])
                act(confT[:, :], C[0:TG * NE, 0:P]).then_inc(s, 1)

            def cls_gelu(e):
                eng.wait_ge(S["cls_ffn1"], e + 1)
                wait(eng, S["cls_ffn2"], e - 1)
                for hc in range(NHC):
                    act(hid[:, e % 2, hc, 0:P], bank[FFN1_BANK[e % 2]][:, hc * P:(hc + 1) * P],
                        ACT.Gelu_apprx_tanh, bias=b1s[:, e, hc:hc + 1]).then_inc(S["cls_gelu"], 1)

            def stats(g, t):
                if t == 0:
                    wait(eng, S["conv_steps"], g * CONVS)
                for j in range(3):
                    eng.wait_ge(S["stat_transposed"], g * 12 + 3 * t + j + 1)
                    a = PAD + t * (GRID // TG)
                    dst = stat[:, 3 * j:3 * j + 3, a:a + GRID // TG]\
                        .rearrange("p s (r w) -> p s r w", w=W9)[:, :, :, 0:NWIN]
                    src = bank[STAT_BANK[(3 * t + j) % 2]][:, 0:3 * P]\
                        .rearrange("p (s r w) -> p s r w", s=3, w=NWIN)
                    act(dst, src).then_inc(S["stat_copied"], 1)

            def gelu(g, e, hcs):
                wait(eng, S["ffn2_done"], g * 8 + e - 1)
                for hc in hcs:
                    eng.wait_ge(S["ffn1_done"], g * 32 + 4 * e + hc + 1)
                    act(hid[:, e % 2, hc, :], bank[FFN1_BANK[hc % 2]][:, :], ACT.Gelu_apprx_tanh,
                        bias=b1s[:, e, hc:hc + 1]).then_inc(S["gelu_done"], 1)

            def mix(g, par, q):
                A, C, D = (bank[b] for b in TOK_BANK)
                if q == 0:
                    eng.wait_ge(S["pooled_transposed"], g + 1)
                    act(h0[:, :, :].rearrange("p t c -> p (t c)"), A[:, :]).then_inc(S["h0_ready"], 1)
                if q == 1:
                    eng.wait_ge(S["hn_transposed"], g + 1)
                    act(hnT[:, :], C[:, :]).then_inc(S["hnT_ready"], 1)
                if q in (2, 3):
                    for t in range(3) if q == 2 else (3,):
                        eng.wait_ge(S["projected"], g * 4 + t + 1)
                        act(xp[:, t, :, :].rearrange("p s c -> p (s c)"), bank[TOK_BANK[t % 3]][:, :])\
                            .then_inc(S["proj_copied"], 1)
                if q == 10:
                    eng.wait_ge(S["xhat_transposed"], g + 1)
                    wait(eng, S["ffn1_done"], g * 32 - 32)
                    act(xnT[:, par, :], A[:, :], ACT.Identity, scale=ln_gc[:, :], bias=ln_bc[:, :])\
                        .then_inc(S["xnT_ready"], 1)
                if q == 12:
                    eng.wait_ge(S["delta_ready"], g + 1)
                    act(th[:, :], delta[:, :], ACT.Tanh, scale=0.5).then_inc(S["tanh_ready"], 1)
                if q == 13:
                    eng.wait_ge(S["conf_transposed"], g + 1)
                    act(confT[:, :], C[0:TG * NE, 0:P]).then_inc(S["confT_ready"], 1)

            def step(i, par, pool, do_mix, experts, finish):
                first = isinstance(i, int) and i == 0
                for q in range(NQ):
                    if do_mix:
                        mix(i - 1, 1 - par, q)
                    if pool and q in (3, 6, 9, 12):
                        stats(i, q // 3 - 1)
                    if first and q % 2 == 0:
                        cls_gelu(q // 2)
                    if q % 2 == 0 and experts:
                        gelu(i - 2, q // 2, range(NHC))

            cls_chain()
            eng.wait_ge(S["weights_loaded"], N_LATE)
            eng.wait_ge(S["pads_zeroed"], 3)
            schedule(eng, step, eng.Fori)

        @block.vector
        def _(eng):
            V = nc.vector

            def carry_wait():
                V.memset(wait_carrier[:, :], 0.0)

            def layer_norm(dst, src, nt, s, base, bn6, mv, rstd):
                for t in range(nt):
                    last = V.bn_stats(bn6[:, t, :], src[:, t, :])
                last.then_inc(s, 1)
                eng.wait_ge(s, base + 1)
                carry_wait()
                for t in range(nt):
                    last = V.bn_aggr(mv[:, t, :], bn6[:, t, :])
                last.then_inc(s, 1)
                eng.wait_ge(s, base + 2)
                eng.wait_ge(s, base + 4)
                for t in range(nt):
                    last = V.tensor_scalar(dst[:, t, :], src[:, t, :], mv[:, t, 0:1], rstd[:, t:t + 1],
                                           ALU.subtract, ALU.mult)
                return last

            def bc_tok(ap, nt):
                return ap.unsqueeze(1).to_broadcast([P, nt, CH])

            def top2(par, nt, src, s, v):
                V.tensor_copy(lg[:, 0:nt, :], src[:, 0:nt * NE].rearrange("p (t e) -> p t e", e=NE)).then_inc(s, 1)
                eng.wait_ge(s, v + 1)
                carry_wait()
                for t in range(nt):
                    last = V.max(top[:, t, :], lg[:, t, :])
                last.then_inc(s, 1)
                eng.wait_ge(s, v + 2)
                carry_wait()
                for t in range(nt):
                    last = V.max_index(top_i[:, t, :], top[:, t, :], lg[:, t, :])
                last.then_inc(s, 1)
                eng.wait_ge(s, v + 3)
                V.tensor_copy(top_f[:, 0:nt, 0:TOPK], top_i[:, 0:nt, 0:TOPK]).then_inc(s, 1)
                return V.tensor_tensor(delta[:, 0:nt], top[:, 0:nt, 0], top[:, 0:nt, 1], ALU.subtract)

            def confidences(par, nt, s, v):
                V.tensor_scalar(c12[:, 0, 0:nt], th[:, 0:nt], 0.5, 0.5, ALU.mult, ALU.add)
                V.tensor_scalar(c12[:, 1, 0:nt], th[:, 0:nt], -0.5, 0.5, ALU.mult, ALU.add).then_inc(s, 1)
                for k in range(TOPK):
                    last = V.tensor_tensor(eq[:, k, 0:nt, :], iota[:, :].unsqueeze(1).to_broadcast([P, nt, NE]),
                                           top_f[:, 0:nt, k].unsqueeze(2).to_broadcast([P, nt, NE]), ALU.is_equal)
                last.then_inc(s, 1)
                eng.wait_ge(s, v + 2)
                for k in range(TOPK):
                    last = V.tensor_tensor(eq[:, k, 0:nt, :], eq[:, k, 0:nt, :],
                                           c12[:, k, 0:nt].unsqueeze(2).to_broadcast([P, nt, NE]), ALU.mult)
                last.then_inc(s, 1)
                eng.wait_ge(s, v + 3)
                return V.tensor_tensor(conf[:, par, 0:nt, :], eq[:, 0, 0:nt, :], eq[:, 1, 0:nt, :], ALU.add)

            def coefficients():
                n = [0]

                def link(ins):
                    n[0] += 1
                    ins.then_inc(S["coef_steps"], 1)
                    eng.wait_ge(S["coef_steps"], n[0])

                for src, dst in ((lambda k: cw[:, k, :], lambda k: coef_r[:, k, :]),
                                 (lambda k: coef_r[:, :, k], lambda k: coef[:, :, k])):
                    V.tensor_copy(dst(0), src(0))
                    V.tensor_copy(dst(4), src(2))
                    link(V.tensor_tensor(dst(1), src(0), src(1), ALU.add))
                    V.tensor_tensor(dst(3), src(1), src(2), ALU.add)
                    link(V.tensor_tensor(dst(2), dst(1), src(2), ALU.add))
                link(V.tensor_scalar(coef[:, :, :], coef[:, :, :], 1.0 / (POOL * POOL), None, ALU.mult))

            def cls_chain():
                A, C, D = (bank[b] for b in TOK_BANK)
                s = S["cls_steps"]
                eng.wait_ge(S["early_loaded"], N_EARLY)
                V.memset(conf[:, 0, :, :], 0.0)
                layer_norm(hn, h0, 1, s, 0, bn6, mv, rstd).then_inc(s, 1)
                eng.wait_ge(s, CLS["spectra_sb"])
                ft, f0 = bank[2], bank[3]
                for k in range(STAGES):
                    cs = slice(k * CH, (k + 1) * CH)
                    V.tensor_tensor(cls_part[:, k, :], ft[:, cs], xp[:, 0, k, :], ALU.mult).then_inc(s, 1)
                    V.tensor_tensor(conv_sum[:, 0, :], f0[:, cs], xp[:, 0, k, :], ALU.mult).then_inc(s, 1)
                    eng.wait_ge(s, CLS[f"convolved{k}"])
                    V.tensor_tensor(xp[:, 0, k + 1, :], conv_sum[:, 0, :], xp[:, 0, k + 1, :], ALU.mult).then_inc(s, 1)
                    eng.wait_ge(s, CLS[f"y{k}"])
                V.tensor_tensor(h1[:, 0, 0, :], h0[:, 0, :], xp[:, 0, STAGES, :], ALU.add).then_inc(s, 1)
                eng.wait_ge(s, CLS["h1"])
                layer_norm(acc[:, 0], h1[:, 0], 1, s, CLS["h1"], bn6, mv, rstd).then_inc(s, 1)
                eng.wait_ge(s, CLS["base"])
                layer_norm(xhat, acc[:, 0], 1, s, CLS["base"], bn6, mv, rstd).then_inc(s, 1)
                eng.wait_ge(s, CLS["logits"])
                top2(0, 1, C, s, CLS["logits"]).then_inc(s, 1)
                eng.wait_ge(s, CLS["tanh"])
                confidences(0, 1, s, CLS["tanh"]).then_inc(s, 1)
                eng.wait_ge(s, CLS["bias"])
                V.tensor_tensor(acc[:, 0, 0, :], D[:, 0:CH], acc[:, 0, 0, :], ALU.add).then_inc(s, 1)

            def cls_add(e):
                eng.wait_ge(S["cls_ffn2"], e + 1)
                if e == 0:
                    eng.wait_ge(S["cls_steps"], CLS["base_b"])
                wait(eng, S["cls_added"], e)
                V.scalar_tensor_tensor(out=acc[:, 0, 0, :], in0=bank[FFN2_BANK][:, 0:CH],
                                       scalar=conf[:, 0, 0, e:e + 1], in1=acc[:, 0, 0, :],
                                       op0=ALU.mult, op1=ALU.add).then_inc(S["cls_added"], 1)

            def window_sums(g, t, part):
                s, v = S["sum_steps"], g * (SUMS * TG) + SUMS * t
                b = xb[:, t % 2]
                if part == 0:
                    eng.wait_ge(x_loaded[t % 2], (g * 2 + t // 2 + 1) * XLOAD)
                    V.tensor_tensor(b[:, 1:4, :], b[:, 1:4, :], b[:, 5:8, :], ALU.add).then_inc(s, 1)
                if part == 1:
                    for n, row in enumerate((1, 3)):
                        eng.wait_ge(s, v + 1 + n)
                        V.tensor_tensor(b[:, 2, :], b[:, 2, :], b[:, row, :], ALU.add).then_inc(s, 1)
                if part == 2:
                    def cols(lo, n):
                        return b[:, 0:5:2, lo * CH:(lo + n) * CH]
                    eng.wait_ge(s, v + 3)
                    V.tensor_tensor(cols(1, 3), cols(1, 3), cols(4, 3), ALU.add).then_inc(s, 1)
                    for n, c in enumerate((2, 3)):
                        eng.wait_ge(s, v + 4 + n)
                        V.tensor_tensor(cols(1, 1), cols(1, 1), cols(c, 1), ALU.add).then_inc(s, 1)

            terms = [(a, b) for a in range(5) for b in range(5) if (a, b) not in ((2, 2), (3, 3))] + [(3, 3)]

            def convolve(g, lo, hi):
                s = S["conv_steps"]
                if lo == 0:
                    eng.wait_ge(S["stat_copied"], g * 12 + 12)
                    wait(eng, S["pooled_transposed"], g)
                    V.tensor_scalar(pooled[:, :], stat[:, 4, PAD:PAD + GRID], coef[:, 2, 2:3], cb[:, :],
                                    ALU.mult, ALU.add).then_inc(s, 1)
                    lo = 1
                for n in range(lo, hi):
                    a, b = terms[n - 1]
                    (ra, di), (rb, dj) = TAPS[a], TAPS[b]
                    i0, rows = max(0, -di), NWIN - abs(di)
                    o = PAD + (i0 + di) * W9 + dj
                    src, dst = stat[:, 3 * ra + rb, o:o + GRID], pooled[:, :]
                    if di:
                        src, dst = (v.rearrange("p (m f) -> p m f", f=NWIN * W9) for v in (src, dst))
                        src = src[:, :, 0:rows * W9]
                        dst = dst[:, :, i0 * W9:(i0 + rows) * W9]
                    res = dst
                    if n == CONVS - 1:
                        src, dst = (v.rearrange("p (r w) -> p r w", w=W9)[:, :, 0:NWIN] for v in (src, dst))
                        res = pooledT[:, :].rearrange("p (r w) -> p r w", w=NWIN)
                    eng.wait_ge(s, g * CONVS + n)
                    V.scalar_tensor_tensor(out=res, in0=src, scalar=coef[:, a, b:b + 1], in1=dst,
                                           op0=ALU.mult, op1=ALU.add).then_inc(s, 1)

            def add_expert(g, par, e):
                eng.wait_ge(S["ffn2_done"], g * 8 + e + 1)
                if e == 0:
                    eng.wait_ge(S["base_ready"], g + 1)
                wait(eng, S["ffn_added"], g * 8 + e)
                for t in range(TG):
                    last = V.scalar_tensor_tensor(out=acc[:, par, t, :], in0=bank[FFN2_BANK][:, t * CH:(t + 1) * CH],
                                                  scalar=conf[:, par, t, e:e + 1], in1=acc[:, par, t, :],
                                                  op0=ALU.mult, op1=ALU.add)
                last.then_inc(S["ffn_added"], 1)

            def finish_group(g, par):
                eng.wait_ge(S["ffn_added"], g * 8 + 8)
                if isinstance(g, int) and g == 0:
                    eng.wait_ge(S["cls_out_steps"], CLS_OUT + 16)
                wait(eng, S["out_stored"], g * (16 * IMG))
                layer_norm(ot, acc[:, par], TG, S["out_norm_steps"], g * 4, bn6o, mvo, rstdo)\
                    .then_inc(S["out_normed"], 1)

            def mix(g, par, q):
                A, C, D = (bank[b] for b in TOK_BANK)
                s = S["norm_steps"]
                if q == 0:
                    eng.wait_ge(S["h0_ready"], g + 1)
                    layer_norm(hn, h0, TG, s, g * NORMS, bn6, mv, rstd).then_inc(S["hn_ready"], 1)
                if q in (4, 6, 8):
                    k = (q - 4) // 2
                    eng.wait_ge(S["spectrum_ready"], g * 3 + k + 1)
                    for n, (z, f) in enumerate(((A, filt_re), (C, filt_im), (A, filt_im), (C, filt_re))):
                        V.tensor_tensor(prod[:, n], z[:, :].rearrange("p (t c) -> p t c", c=CH),
                                        bc_tok(f[:, k, :], TG), ALU.mult).then_inc(S["product_ready"], 1)
                if q in (5, 7, 9):
                    k = (q - 5) // 2
                    eng.wait_ge(S["filtered"], g * 3 + k + 1)
                    V.tensor_tensor(conv_sum[:, :, :], D[:, :].rearrange("p (t c) -> p t c", c=CH),
                                    bc_tok(cls_part[:, k, :], TG), ALU.add).then_inc(S["conv_summed"], 1)
                    eng.wait_ge(S["conv_summed"], g * 3 + k + 1)
                    V.tensor_tensor(xp[:, :, k + 1, :], conv_sum[:, :, :], xp[:, :, k + 1, :], ALU.mult)\
                        .then_inc(S["y_ready"], 1)
                if q == 9:
                    eng.wait_ge(S["y_ready"], g * 3 + 3)
                    if isinstance(g, int) and g == 0:
                        eng.wait_ge(S["cls_out_steps"], CLS_OUT)
                    wait(eng, S["out_summed"], g - 1)
                    V.tensor_tensor(h1[:, par], h0[:, :, :], xp[:, :, STAGES, :], ALU.add)\
                        .then_inc(S["h1_ready"], 1)
                    eng.wait_ge(S["h1_ready"], g + 1)
                    layer_norm(acc[:, par], h1[:, par], TG, s, g * NORMS + 4, bn6, mv, rstd)\
                        .then_inc(S["base_normed"], 1)
                    eng.wait_ge(S["base_normed"], g + 1)
                    layer_norm(xhat, acc[:, par], TG, s, g * NORMS + 8, bn6, mv, rstd)\
                        .then_inc(S["xhat_ready"], 1)
                if q == 11:
                    eng.wait_ge(S["logits_ready"], g + 1)
                    top2(par, TG, C, S["gate_steps"], g * 4).then_inc(S["delta_ready"], 1)
                if q == 12:
                    eng.wait_ge(S["tanh_ready"], g + 1)
                    confidences(par, TG, S["mask_steps"], g * 3).then_inc(S["conf_ready"], 1)
                if q == 14:
                    eng.wait_ge(S["bias_ready"], g + 1)
                    V.tensor_tensor(acc[:, par], D[:, :].rearrange("p (t c) -> p t c", c=CH), acc[:, par], ALU.add)\
                        .then_inc(S["base_ready"], 1)

            def step(i, par, pool, do_mix, experts, finish):
                first = isinstance(i, int) and i == 0
                second = isinstance(i, int) and i == 1
                for q in range(NQ):
                    if first and q >= 2 and q % 2 == 0:
                        cls_add(q // 2 - 1)
                    if second and q == 0:
                        cls_add(NE - 1)
                        eng.wait_ge(S["cls_added"], NE)
                        layer_norm(ot, acc[:, 0], 1, S["cls_out_steps"], 0, bn6o, mvo, rstdo)\
                            .then_inc(S["cls_out_steps"], 1)
                    if q == 0 and finish:
                        add_expert(i - 3, 1 - par, 6)
                    if q == 2 and finish:
                        add_expert(i - 3, 1 - par, 7)
                        finish_group(i - 3, 1 - par)
                    if q >= 4 and q % 2 == 0 and experts:
                        add_expert(i - 2, par, q // 2 - 2)
                    if pool and q < 12:
                        window_sums(i, q // 3, q % 3)
                    if pool and q >= 13:
                        convolve(i, *((0, 9), (9, 17), (17, 25))[q - 13])
                    if do_mix:
                        mix(i - 1, 1 - par, q)

            cls_chain()
            coefficients()
            schedule(eng, step, eng.Fori)


def kernel(x, cls_tok, L0_tok_conv_w, L0_tok_conv_b, L0_attn_W_proj, L0_attn_W_filt, L0_ffn_Wg, L0_ffn_W1,
           L0_ffn_b1, L0_ffn_W2, L0_ffn_b2, L0_ffn_ln_g, L0_ffn_ln_b, L0_ffn_out_g, L0_ffn_out_b):
    import concourse.bacc as bacc
    from concourse.bass_utils import run_bass_kernel_spmd

    a = np.asarray
    b2 = a(L0_ffn_b2)
    b2_blocks = np.zeros((TG, NE, TG, CH), b2.dtype)
    for t in range(TG):
        b2_blocks[t, :, t, :] = b2
    arrays = {
        "x": a(x),
        "cls_tok": a(cls_tok),
        "conv_w": a(L0_tok_conv_w).reshape(3, 3, CH).transpose(2, 0, 1),
        "conv_b": a(L0_tok_conv_b).reshape(CH, 1),
        "w_proj": a(L0_attn_W_proj).transpose(0, 2, 1).reshape(CH, -1),
        "w_filt": a(L0_attn_W_filt).transpose(0, 2, 1).reshape(CH, -1),
        "w_gate": a(L0_ffn_Wg),
        "w1": a(L0_ffn_W1).transpose(1, 0, 2),
        "b1": a(L0_ffn_b1).reshape(NE, NHC, P).transpose(2, 0, 1),
        "w2": a(L0_ffn_W2).reshape(NE, NHC, P, CH).transpose(2, 0, 1, 3),
        "b2_blocks": b2_blocks.reshape(TG * NE, TG, CH),
        "ln_g": a(L0_ffn_ln_g).reshape(CH, 1),
        "ln_b": a(L0_ffn_ln_b).reshape(CH, 1),
        "out_g": a(L0_ffn_out_g),
        "out_b": a(L0_ffn_out_b),
        **shape_constants(),
    }
    arrays = {f"in_{n}": np.ascontiguousarray(v) for n, v in arrays.items()}
    nc = bacc.Bacc("TRN2", target_bir_lowering=False, num_devices=1)
    args = [nc.dram_tensor(n, v.shape, mybir.dt.from_np(v.dtype), kind="ExternalInput").ap()
            for n, v in arrays.items()]
    out = nc.dram_tensor("out_dram", (B, T + 1, CH), F32, kind="ExternalOutput").ap()
    build(nc, *args, out)
    r = run_bass_kernel_spmd(nc, [arrays], core_ids=[0])
    return r.results[0]["out_dram"]
```

```python
from contextlib import ExitStack

import numpy as np
import concourse.bass as bass
from concourse import mybir

P = 128
B, HW, CH = 128, 64, 128
POOL = 8
NWIN = HW // POOL
T = NWIN * NWIN
STAGES = 3
NE, HID, TOPK = 8, 512, 2
NHC = HID // P
IMG = P // T
TG = 4
NG = B // (IMG * TG)
N = TG * P
NFFT = 2 * T
EPS = 1e-5
ROW = POOL * CH
W9 = NWIN + 1
GRID = IMG * TG * NWIN * W9
PAD = 2
NST = 9
NQ = 16
LOOKBACK = 4

F32 = mybir.dt.float32
F32R = mybir.dt.float32r
U32 = mybir.dt.uint32
ALU = mybir.AluOpType
ACT = mybir.ActivationFunctionType

ROW_SLOT = {0: 0, 1: 1, 2: 2, 3: 3, 7: 4, 4: 5, 5: 6, 6: 7}
STAT_ROW = (0, 2, 4)
STAT_COL = (0, 1, 7)
TAPS = ((2, -1), (0, 0), (1, 0), (2, 0), (0, 1))


def shape_constants():
    half = CH // 2
    freqs = (10000.0 ** (-np.arange(half, dtype=np.float32) / half)).astype(np.float32)
    phi = np.arange(T + 1, dtype=np.float32)[:, None] * freqs[None, :]
    pe = np.concatenate([np.sin(phi), np.cos(phi)], axis=-1).astype(np.float64)
    theta = 2 * np.pi * np.outer(np.arange(NFFT), np.arange(T)) / NFFT
    cos, sin = np.cos(theta), np.sin(theta)
    dft = np.stack([np.concatenate([cos.T, sin.T], 0), np.concatenate([-sin.T, cos.T], 0)], 1)
    back_re = np.concatenate([cos, sin], 1) / NFFT
    back_im = np.concatenate([-sin, cos], 1) / NFFT
    idft = np.stack([back_re, back_im], 1)
    pe_mats = np.stack([pe[:T].T @ cos.T, -(pe[:T].T @ sin.T),
                        np.concatenate([pe[1:T + 1].T] * IMG, 1),
                        np.repeat(pe[0][:, None], P, 1)], 1)
    return {
        "ident": np.eye(P, dtype=np.float32),
        "dft": dft.reshape(P, -1).astype(np.float32),
        "idft": idft.reshape(P, -1).astype(np.float32),
        "pe_mats": pe_mats.reshape(P, -1).astype(np.float32),
        "iota": np.tile(np.arange(NE, dtype=np.float32), (P, 1)),
    }


def build(nc, x, cls_tok, conv_w, conv_b, w_proj, w_filt, w_gate, w1, b1, w2, b2_blocks,
          ln_g, ln_b, out_g, out_b, ident_d, dft_d, idft_d, pe_mats_d, iota_d, out):
    ctx = ExitStack()
    with ctx:
        def sb(name, shape, dt=F32):
            return ctx.enter_context(nc.sbuf_tensor(name, shape, dt))

        def sem(name):
            return ctx.enter_context(nc.semaphore(name))

        def wait(eng, s, value):
            if not isinstance(value, int) or value > 0:
                eng.wait_ge(s, value)

        ident = sb("ident", [P, P])
        dft = sb("dft_sb", [P, 2, P])
        idft = sb("idft_sb", [P, 2, P])
        iota = sb("iota_sb", [P, NE])
        wp = sb("wp", [P, (STAGES + 1) * CH])
        wg = sb("wg", [P, NE])
        w1_hi = sb("w1_hi", [P, NE, HID], F32R)
        w1_lo = sb("w1_lo", [P, NE, HID], F32R)
        w2s = sb("w2s", [P, NE, NHC, CH])
        b1s = sb("b1s", [P, NE, NHC])
        b2s = sb("b2s", [TG * NE, TG, CH])
        ln_gc = sb("ln_gc", [P, 1])
        ln_bc = sb("ln_bc", [P, 1])
        out_gr = sb("out_gr", [P, CH])
        out_br = sb("out_br", [P, CH])
        cw = sb("cw", [P, 3, 3])
        cb = sb("cb", [P, 1])
        coef_r = sb("coef_r", [P, 5, 3])
        coef = sb("coef", [P, 5, 5])
        filt_re = sb("filt_re", [P, STAGES, CH])
        filt_im = sb("filt_im", [P, STAGES, CH])
        cls_part = sb("cls_part", [P, STAGES, CH])

        xb = sb("xb", [P, 2, POOL, ROW])
        stat = sb("stat", [P, NST, PAD + GRID + W9 + 1])
        pooled = sb("pooled", [P, 2, GRID])
        h0 = sb("h0", [P, TG, CH])
        hn = sb("hn", [P, TG, CH])
        by_ch = sb("by_ch", [P, N])
        xp = sb("xp", [P, TG, STAGES + 1, CH])
        prod = sb("prod", [P, 4, TG, CH])
        conv_sum = prod[:, 1]
        pe_mats = prod[:, 0].rearrange("p t c -> p (t c)").rearrange("p (a b) -> p a b", a=4)
        wf = prod[:, 1].rearrange("p t c -> p (t c)")[:, 0:STAGES * CH]
        h1 = sb("h1", [P, 2, TG, CH])
        acc = sb("acc", [P, 2, TG, CH])
        xhat = hn
        xn_hi = sb("xn_hi", [P, 2, N], F32R)
        xn_lo = sb("xn_lo", [P, N], F32R)
        scaled = sb("scaled", [P, TG, CH])
        lg = sb("lg", [P, TG, NE])
        top = sb("top", [P, TG, 8])
        top_i = sb("top_i", [P, TG, 8], U32)
        top_f = sb("top_f", [P, TG, 8])
        delta = sb("delta", [P, TG])
        th = sb("th", [P, TG])
        c12 = sb("c12", [P, 2, TG])
        eq = sb("eq", [P, 2, TG, NE])
        conf = sb("conf", [P, 2, TG, NE])
        confT = sb("confT", [TG * NE, P])
        hid = sb("hid", [P, 2, NHC, N])
        w1_stage = hid[:, :, :, :].rearrange("p a b n -> p (a b n)").rearrange("p (e h) -> p e h", e=NE)
        ot = sb("ot", [P, TG, CH])
        neg_half = sb("neg_half", [P, 2, TG])
        wait_carrier = sb("wait_carrier", [P, 1])
        eps_t = sb("eps_t", [P, TG])
        shift = sb("shift", [P, 2, TG])
        bn6 = sb("bn6", [P, TG, 6])
        mv = sb("mv", [P, TG, 2])
        rstd = sb("rstd", [P, 2, TG])
        bn6o = sb("bn6o", [P, TG, 6])
        mvo = sb("mvo", [P, TG, 2])
        rstdo = sb("rstdo", [P, 2, TG])
        shifto = sb("shifto", [P, 2, TG])
        cls_h1 = h1[:, 1, 0:1, :]
        cls_acc = acc[:, 1, 0:1, :]
        cls_conf = conf[:, 1]

        bank = [ctx.enter_context(nc.psum_tensor(f"bank{i}", [P, N], F32)) for i in range(8)]
        FFN1_BANK, FFN2_BANK, STAT_BANK, TOK_BANK = (0, 1, 2), 3, 4, (5, 6, 7)

        CLS_BANK = (FFN2_BANK, FFN1_BANK[2])

        names = """early_loaded weights_loaded pads_zeroed coef_steps
            row_sums col_sums stat_transposed stat_copied conv_steps
            pooled_transposed h0_ready norm_steps hn_ready hn_transposed hnT_ready
            projected proj_copied spectrum_ready product_ready product_summed filtered conv_summed y_ready
            h1_ready base_normed xhat_ready xhat_transposed xnT_ready xn_hi_ready xn_lo_ready logits_ready
            w1_split expert_scaled
            gate_steps delta_ready tanh_ready mask_steps conf_ready conf_transposed confT_ready
            bias_ready base_ready ffn1_done gelu_done ffn2_done ffn_added
            out_norm_steps out_normed out_scaled out_summed out_stored
            cls_steps cls_ffn1 cls_gelu cls_ffn2 cls_added cls_out_steps""".split()
        S = {n: sem(n) for n in names}
        CHUNKS = NE * NHC

        def chunks_out(n):
            return n - 2 if n > 1 else n - 1

        x_loaded = [sem("x_loaded0"), sem("x_loaded1")]
        XLOAD = 16 * POOL
        HALF = 25
        CONVS = 2 * HALF + 1
        NORM = 5
        CLS_OUT = NORM + 4

        cls_order = ["n1", "n2", "n3", "n4", "n5", "normed", "transposed", "hnT", "projected", "xp",
                     "spectra", "spectra_sb"]
        cls_order += [f"{n}{k}" for k in range(STAGES) for n in ("part", "convolved", "y")]
        cls_order += ["h1", "m1", "m2", "m3", "m4", "m5", "base", "xhat", "xhat_t", "xnT", "xn_hi", "xn_lo",
                      "logits", "lg", "top", "top_i", "top_f", "delta", "tanh", "c12", "eq", "masked",
                      "conf", "conf_t", "confT", "bias", "base_b"]
        CLS = {n: k + 1 for k, n in enumerate(cls_order)}

        block = ctx.enter_context(nc.Block())

        def due(i, q, slot):
            if slot % NQ != q:
                return None
            g = i - slot // NQ
            return None if isinstance(g, int) and not 0 <= g < NG else g

        def schedule(step, Fori):
            for i in range(LOOKBACK):
                step(i, i % 2)
            with Fori(LOOKBACK // 2, NG // 2) as pair:
                step(pair * 2, 0)
                step(pair * 2 + 1, 1)
            for i in range(NG, NG + LOOKBACK - 1):
                step(i, i % 2)

        TILE_SLOT = (0, 5, 8, 12)
        STAT_SLOT = (((3, "last"), (4, "last"), (5, "within")), ((8, "last"), (9, "within"), (9, "last")),
                     ((11, "last"), (12, "last"), (13, "within")), ((15, "last"), (16, "last"), (17, "within")))
        CLS_FFN = 16

        def at_step(i, n):
            return isinstance(i, int) and i == n

        def at_slot(i, q, n):
            return isinstance(i, int) and i * NQ + q == n

        @block.sync
        def _(eng):
            early = [(h0[:, 0, :], cls_tok[0, 0, :].partition_broadcast(P)),
                     (ident[:, :], ident_d), (wp[:, :], w_proj), (wf, w_filt),
                     (pe_mats, pe_mats_d.rearrange("p (a b) -> p a b", a=4)),
                     (wg[:, :], w_gate), (iota[:, :], iota_d), (cw[:, :, :], conv_w), (cb[:, :], conv_b),
                     (ln_gc[:, :], ln_g), (ln_bc[:, :], ln_b),
                     (b2s[:, :, :], b2_blocks)]
            late = [(dft[:, :, :], dft_d.rearrange("p (a b) -> p a b", a=2)),
                    (idft[:, :, :], idft_d.rearrange("p (a b) -> p a b", a=2)),
                    (b1s[:, :, :], b1),
                    (out_gr[:, :], out_g.partition_broadcast(P)), (out_br[:, :], out_b.partition_broadcast(P)),
                    (w1_stage, w1), (w2s[:, :, :, :], w2)]
            for dst, src in early:
                eng.dma_start(dst, src).then_inc(S["early_loaded"], 16)

            def load_tile(g, t):
                images = bass.ds(g * (IMG * TG) + IMG * t, IMG)
                row = x.rearrange("b (i r) (j w) c -> b i r j (w c)", r=POOL, w=POOL)
                last = g * TG + t - 2
                for lot, ready, value in (((4, 5, 6), "row_sums", last * 3 + 1),
                                          ((1, 3), "row_sums", last * 3 + 3),
                                          ((2, 0, 7), "stat_transposed", last * 3 + 3)):
                    if not isinstance(last, int) or last >= 0:
                        eng.wait_ge(S[ready], value)
                    for r in lot:
                        eng.dma_start(xb[:, t % 2, ROW_SLOT[r], :],
                                      row[:, :, r][images].rearrange("b i j c -> (b i) j c"))\
                           .then_inc(x_loaded[t % 2], 16)

            def step(i, par):
                for t in range(TG):
                    g = due(i, 0, 0)
                    if g is not None:
                        load_tile(g, t)
                    if at_step(i, 0) and t == 1:
                        for dst, src in late:
                            eng.dma_start(dst, src).then_inc(S["weights_loaded"], 16)
                if at_step(i, 2):
                    eng.wait_ge(S["cls_out_steps"], CLS_OUT)
                    eng.dma_start(out[:, 0, :], ot[:, 0, :]).then_inc(S["cls_out_steps"], 16)

            schedule(step, eng.Fori)
            eng.wait_ge(S["cls_out_steps"], CLS_OUT + 16)
            eng.wait_ge(S["out_stored"], 16 * IMG * NG)

        N_EARLY, N_LATE = 16 * 12, 16 * 7

        @block.gpsimd
        def _(eng):
            eng.memset(neg_half[:, :, :], -0.5).then_inc(S["pads_zeroed"], 1)
            eng.memset(eps_t[:, :], EPS).then_inc(S["pads_zeroed"], 1)
            eng.memset(stat[:, :, :], 0.0).then_inc(S["pads_zeroed"], 1)
            eng.wait_ge(S["pads_zeroed"], 3)

            def affine(o, h, nt, ready, ready_value, scaled, scaled_value, summed):
                eng.wait_ge(ready, ready_value)
                eng.tensor_tensor(o, o, out_gr[:, :].unsqueeze(1).to_broadcast([P, nt, CH]), ALU.mult)\
                   .then_inc(scaled, 1)
                eng.wait_ge(scaled, scaled_value)
                eng.tensor_tensor(o, o, out_br[:, :].unsqueeze(1).to_broadcast([P, nt, CH]), ALU.add)\
                   .then_inc(scaled, 1)
                eng.wait_ge(scaled, scaled_value + 1)
                eng.tensor_tensor(o, o, h, ALU.add).then_inc(summed, 1)

            def inverse_std(s, base, nt, mv, rstd, shift, twice=False):
                n = 2 if twice else 1
                eng.wait_ge(s, base + 2)
                eng.tensor_tensor(rstd[:, 0, 0:nt], mv[:, 0:nt, 1], eps_t[:, 0:nt], ALU.add)
                if twice:
                    eng.tensor_scalar(rstd[:, 1, 0:nt], mv[:, 0:nt, 1], 1.0 + EPS, EPS * EPS,
                                      ALU.mult, ALU.add)
                eng.tensor_scalar(shift[:, 0:n, 0:nt], mv[:, 0:nt, 0].unsqueeze(1).to_broadcast([P, n, nt]),
                                  -1.0, None, ALU.mult).then_inc(s, 1)
                eng.wait_ge(s, base + 3)
                eng.tensor_tensor(rstd[:, 0:n, 0:nt], rstd[:, 0:n, 0:nt], neg_half[:, 0:n, 0:nt], ALU.pow)\
                   .then_inc(s, 1)
                eng.wait_ge(s, base + 4)
                eng.tensor_tensor(shift[:, 0:n, 0:nt], rstd[:, 0:n, 0:nt], shift[:, 0:n, 0:nt], ALU.mult)\
                   .then_inc(s, 1)

            def add_expert(g, par, e):
                eng.wait_ge(S["expert_scaled"], g * NE + e + 1)
                if e == 0:
                    eng.wait_ge(S["base_ready"], g + 1)
                wait(eng, S["ffn_added"], g * NE + e)
                eng.tensor_tensor(acc[:, par], acc[:, par], scaled[:, :, :], ALU.add).then_inc(S["ffn_added"], 1)

            def sum_products(g, k):
                for n, op in ((0, ALU.subtract), (2, ALU.add)):
                    eng.wait_ge(S["product_ready"], g * 12 + 4 * k + n + 2)
                    eng.tensor_tensor(prod[:, n], prod[:, n], prod[:, n + 1], op).then_inc(S["product_summed"], 1)

            def products(i, q):
                for k in range(STAGES):
                    g = due(i, q, 25 + 3 * k)
                    if g is not None:
                        sum_products(g, k)

            def column_sums(g, t, part):
                s, v, b = S["col_sums"], g * (3 * TG) + 3 * t, xb[:, t % 2]

                def cols(lo, n):
                    return b[:, 0:5:2, lo * CH:(lo + n) * CH]
                if part == 0:
                    eng.wait_ge(S["row_sums"], v + 3)
                    eng.tensor_tensor(cols(1, 3), cols(1, 3), cols(4, 3), ALU.add).then_inc(s, 1)
                else:
                    for n, c in enumerate((2, 3)):
                        eng.wait_ge(s, v + 1 + n)
                        eng.tensor_tensor(cols(1, 1), cols(1, 1), cols(c, 1), ALU.add).then_inc(s, 1)

            def step(i, par):
                for q in range(NQ):
                    if at_step(i, 0) and q == 0:
                        inverse_std(S["cls_steps"], 0, 1, mv, rstd, shift)
                    if at_step(i, 0) and q == 2:
                        inverse_std(S["cls_steps"], CLS["h1"], 1, mv, rstd, shift, True)
                    if at_slot(i, q, CLS_FFN + 3 + 2 * NE):
                        inverse_std(S["cls_out_steps"], 0, 1, mvo, rstdo, shifto)
                    if at_slot(i, q, CLS_FFN + 6 + 2 * NE):
                        eng.wait_ge(S["weights_loaded"], N_LATE)
                        affine(ot[:, 0:1, :], cls_h1[:, :, :], 1, S["cls_out_steps"], NORM + 1,
                               S["cls_out_steps"], NORM + 2, S["cls_out_steps"])
                    for slot, place, n_norm in ((21, 0, 1), (34, NORM, 2)):
                        g = due(i, q, slot)
                        if g is not None:
                            inverse_std(S["norm_steps"], g * (2 * NORM) + place, TG, mv, rstd, shift, n_norm == 2)
                    for e in range(NE):
                        g = due(i, q, 42 + 2 * e)
                        if g is not None:
                            add_expert(g, (par - (42 + 2 * e) // NQ) % 2, e)
                    g = due(i, q, 58)
                    if g is not None:
                        inverse_std(S["out_norm_steps"], g * NORM, TG, mvo, rstdo, shifto)
                    for t in range(TG):
                        for part in range(2):
                            g = due(i, q, TILE_SLOT[t] + 1 + part)
                            if g is not None:
                                column_sums(g, t, part)
                    products(i, q)
                    g = due(i, q, 60)
                    if g is not None:
                        affine(ot[:, :, :], h1[:, 1 - par, :, :], TG, S["out_normed"], g + 1,
                               S["out_scaled"], g * 2 + 1, S["out_summed"])

            schedule(step, eng.Fori)

        @block.tensor
        def _(eng):
            A, C, D = (bank[b] for b in TOK_BANK)

            def mm(o, lhsT, rhs, start=True, stop=True):
                return nc.tensor.matmul(o, lhsT, rhs, start=start, stop=stop)

            def transpose_tiles(o, src, nt):
                for t in range(nt):
                    last = nc.tensor.transpose(o[:, t * P:(t + 1) * P], src(t), ident[:, :])
                return last

            def gate(o, nt):
                for t in range(nt):
                    last = mm(o[:, t * NE:(t + 1) * NE], by_ch[:, t * P:(t + 1) * P], wg[:, :])
                return last

            def hidden(o, e, hc, par, cols):
                h = slice(hc * P, (hc + 1) * P)
                mm(o, w1_hi[:, e, h], xn_hi[:, par, cols], True, False)
                mm(o, w1_hi[:, e, h], xn_lo[:, cols], False, False)
                return mm(o, w1_lo[:, e, h], xn_hi[:, par, cols], False, True)

            def cls_chain(q):
                s = S["cls_steps"]
                if q == 1:
                    eng.wait_ge(S["early_loaded"], N_EARLY)
                    eng.wait_ge(s, CLS["normed"])
                    nc.tensor.transpose(C[:, 0:P], hn[:, 0, :], ident[:, :]).then_inc(s, 1)
                    eng.wait_ge(s, CLS["hnT"])
                    mm(A[:, :], by_ch[:, 0:P], wp[:, :]).then_inc(s, 1)
                    eng.wait_ge(s, CLS["xp"])
                    for n, b in enumerate((bank[0], bank[1], bank[2], A)):
                        last = mm(b[:, 0:STAGES * CH], pe_mats[:, n, :], wf)
                    last.then_inc(s, 1)
                if q == 3:
                    eng.wait_ge(s, CLS["xhat"])
                    nc.tensor.transpose(A[:, 0:P], xhat[:, 0, :], ident[:, :]).then_inc(s, 1)
                if q == 4:
                    eng.wait_ge(s, CLS["xn_lo"])
                    gate(C, 1).then_inc(s, 1)
                if q == 6:
                    eng.wait_ge(s, CLS["conf"])
                    nc.tensor.transpose(C[0:TG * NE, 0:P], cls_conf[:, :, :].rearrange("p t e -> p (t e)"),
                                        ident[:, :]).then_inc(s, 1)
                    eng.wait_ge(s, CLS["confT"])
                    mm(D[:, 0:P], confT[0:NE, :], b2s[0:NE, 0, :]).then_inc(s, 1)

            def cls_expert(e, second):
                if not second:
                    if e == 0:
                        eng.wait_ge(S["weights_loaded"], N_LATE)
                        eng.wait_ge(S["w1_split"], 2)
                    wait(eng, S["cls_gelu"], 4 * (e - 1))
                    for hc in range(NHC):
                        last = hidden(bank[FFN1_BANK[e % 2]][:, hc * P:(hc + 1) * P], e, hc, 0, slice(0, P))
                    last.then_inc(S["cls_ffn1"], 1)
                else:
                    eng.wait_ge(S["cls_gelu"], 4 * e + 4)
                    wait(eng, S["cls_added"], e - 1)
                    for hc in range(NHC):
                        last = mm(bank[CLS_BANK[e % 2]][:, 0:CH], hid[:, e % 2, hc, 0:P], w2s[:, e, hc, :],
                                  hc == 0, hc == NHC - 1)
                    last.then_inc(S["cls_ffn2"], 1)

            def stats(g, t, j):
                if j == 0:
                    eng.wait_ge(S["col_sums"], g * (3 * TG) + 3 * (t + 1))
                wait(eng, S["stat_copied"], g * 12 + 3 * t + j)
                for k in range(3):
                    a = STAT_COL[k] * CH
                    last = nc.tensor.transpose(bank[STAT_BANK][:, k * P:(k + 1) * P],
                                               xb[:, t % 2, STAT_ROW[j], a:a + CH], ident[:, :])
                last.then_inc(S["stat_transposed"], 1)

            def row_stats(i, q, here):
                for t in range(TG):
                    for j in range(3):
                        slot, place = STAT_SLOT[t][j]
                        g = due(i, q, slot)
                        if g is not None and place == here:
                            stats(g, t, j)

            def ffn1(g, par, e, hcs):
                for hc in hcs:
                    if e == 0 and hc == 0:
                        eng.wait_ge(S["xn_lo_ready"], g + 1)
                    n = NHC * e + hc
                    wait(eng, S["gelu_done"], g * CHUNKS + chunks_out(n))
                    hidden(bank[FFN1_BANK[n % 3]][:, :], e, hc, par, slice(0, N)).then_inc(S["ffn1_done"], 1)

            def ffn2(g, e):
                eng.wait_ge(S["gelu_done"], g * CHUNKS + NHC * e + NHC)
                wait(eng, S["expert_scaled"], g * NE + e)
                for t in range(TG):
                    for hc in range(NHC):
                        last = mm(bank[FFN2_BANK][:, t * CH:(t + 1) * CH], hid[:, e % 2, hc, t * P:(t + 1) * P],
                                  w2s[:, e, hc, :], hc == 0, hc == NHC - 1)
                last.then_inc(S["ffn2_done"], 1)

            def chain(i, par, q, place):
                for k in range(STAGES):
                    g = due(i, q, 25 + 3 * k)
                    if g is not None and place == "within":
                        if k == 0:
                            eng.wait_ge(S["proj_copied"], g * 4 + 4)
                        else:
                            eng.wait_ge(S["y_ready"], g * 3 + k)
                        mm(A[:, :], dft[:, 0, :], xp[:, :, k, :]).then_inc(S["spectrum_ready"], 1)
                        mm(C[:, :], dft[:, 1, :], xp[:, :, k, :]).then_inc(S["spectrum_ready"], 1)
                    g = due(i, q, 27 + 3 * k)
                    if g is not None and place == ("first" if k == STAGES - 1 else "within"):
                        for m in range(2):
                            eng.wait_ge(S["product_summed"], g * 6 + 2 * k + m + 1)
                            last = mm(D[:, :], idft[:, m, :], prod[:, 2 * m, :, :], m == 0, m == 1)
                        last.then_inc(S["filtered"], 1)
                g = due(i, q, 21)
                if g is not None and place == "within":
                    eng.wait_ge(S["conv_steps"], g * CONVS + CONVS)
                    wait(eng, S["xnT_ready"], g)
                    transpose_tiles(A, lambda t: by_ch[:, t * P:(t + 1) * P], TG)\
                        .then_inc(S["pooled_transposed"], 1)
                g = due(i, q, 39)
                if g is not None and place == "first":
                    eng.wait_ge(S["conf_ready"], g + 1)
                    nc.tensor.transpose(C[0:TG * NE, 0:P], conf[:, par, :, :].rearrange("p t e -> p (t e)"),
                                        ident[:, :]).then_inc(S["conf_transposed"], 1)
                if g is not None and place == "last":
                    eng.wait_ge(S["confT_ready"], g + 1)
                    mm(D[:, :], confT[:, :], b2s[:, :, :]).then_inc(S["bias_ready"], 1)
                g = due(i, q, 23)
                if g is not None and place == "within":
                    eng.wait_ge(S["hn_ready"], g + 1)
                    wait(eng, S["confT_ready"], g)
                    transpose_tiles(C, lambda t: hn[:, t, :], TG).then_inc(S["hn_transposed"], 1)
                g = due(i, q, 24)
                if g is not None and place == "first":
                    eng.wait_ge(S["hnT_ready"], g + 1)
                    for t in range(TG):
                        if t == 2:
                            wait(eng, S["base_ready"], g)
                        if t == 3:
                            eng.wait_ge(S["proj_copied"], g * 4 + 1)
                        mm(bank[TOK_BANK[t % 3]][:, :], by_ch[:, t * P:(t + 1) * P], wp[:, :])\
                            .then_inc(S["projected"], 1)
                g = due(i, q, 35)
                if g is not None and place == "last":
                    eng.wait_ge(S["xhat_ready"], g + 1)
                    transpose_tiles(A, lambda t: xhat[:, t, :], TG).then_inc(S["xhat_transposed"], 1)
                g = due(i, q, 36)
                if g is not None and place == "last":
                    eng.wait_ge(S["xnT_ready"], g + 1)
                    gate(C, TG).then_inc(S["logits_ready"], 1)

            def step(i, par):
                for q in range(NQ):
                    if at_step(i, 0):
                        cls_chain(q)
                    chain(i, par, q, "first")
                    for e in range(NE):
                        slot = 37 + 2 * e
                        g = due(i, q, slot)
                        if g is not None:
                            ffn1(g, (par - slot // NQ) % 2, e, (0, 1))
                    chain(i, par, q, "within")
                    row_stats(i, q, "within")
                    for e in range(NE):
                        slot = 37 + 2 * e
                        g = due(i, q, slot)
                        if g is not None:
                            ffn1(g, (par - slot // NQ) % 2, e, (2, 3))
                        g = due(i, q, 40 + 2 * e)
                        if g is not None:
                            ffn2(g, e)
                    row_stats(i, q, "last")
                    chain(i, par, q, "last")
                    for e in range(NE):
                        if at_slot(i, q, CLS_FFN + 2 * e):
                            cls_expert(e, False)
                        if at_slot(i, q, CLS_FFN + 1 + 2 * e):
                            cls_expert(e, True)

            schedule(step, eng.Fori)

        @block.scalar
        def _(eng):
            A, C, D = (bank[b] for b in TOK_BANK)

            def act(o, i, f=ACT.Copy, **kw):
                return nc.scalar.activation(o, i, f, **kw)

            def normalise(dst, src, rstd, shift, n=0):
                for t in range(TG):
                    last = act(dst[:, t, :], src[:, t, :], ACT.Identity, scale=rstd[:, n, t:t + 1],
                               bias=shift[:, n, t:t + 1])
                return last

            def cls_chain(q):
                s = S["cls_steps"]
                if q == 1:
                    eng.wait_ge(S["early_loaded"], N_EARLY)
                    eng.wait_ge(s, CLS["transposed"])
                    act(by_ch[:, 0:P], C[:, 0:P]).then_inc(s, 1)
                    eng.wait_ge(s, CLS["projected"])
                    act(xp[:, 0, :, :].rearrange("p s c -> p (s c)"), A[:, :]).then_inc(s, 1)
                    eng.wait_ge(s, CLS["spectra"])
                    act(filt_re[:, :, :].rearrange("p s c -> p (s c)"), bank[0][:, 0:STAGES * CH])
                    act(filt_im[:, :, :].rearrange("p s c -> p (s c)"), bank[1][:, 0:STAGES * CH]).then_inc(s, 1)
                if q == 3:
                    eng.wait_ge(s, CLS["xhat_t"])
                    for dst in (by_ch[:, 0:P], xn_hi[:, 0, 0:P]):
                        act(dst, A[:, 0:P], ACT.Identity, scale=ln_gc[:, :], bias=ln_bc[:, :]).then_inc(s, 1)
                if q == 5:
                    eng.wait_ge(s, CLS["delta"])
                    act(th[:, 0:1], delta[:, 0:1], ACT.Tanh, scale=0.5).then_inc(s, 1)
                if q == 6:
                    eng.wait_ge(s, CLS["conf_t"])
                    act(confT[:, :], C[0:TG * NE, 0:P]).then_inc(s, 1)
                if q == 8:
                    eng.wait_ge(S["weights_loaded"], N_LATE)
                    act(w1_hi[:, :, :], w1_stage).then_inc(S["w1_split"], 1)

            def cls_gelu(e):
                eng.wait_ge(S["cls_ffn1"], e + 1)
                wait(eng, S["cls_ffn2"], e - 1)
                for hc in range(NHC):
                    act(hid[:, e % 2, hc, 0:P], bank[FFN1_BANK[e % 2]][:, hc * P:(hc + 1) * P],
                        ACT.Gelu_apprx_tanh, bias=b1s[:, e, hc:hc + 1]).then_inc(S["cls_gelu"], 1)

            def stats(g, t, j):
                if j == 0:
                    wait(eng, S["conv_steps"], g * CONVS + (t // 2 + 1) * HALF - CONVS)
                eng.wait_ge(S["stat_transposed"], g * 12 + 3 * t + j + 1)
                a = PAD + t * (GRID // TG)
                dst = stat[:, 3 * j:3 * j + 3, a:a + GRID // TG]\
                    .rearrange("p s (r w) -> p s r w", w=W9)[:, :, :, 0:NWIN]
                src = bank[STAT_BANK][:, 0:3 * P].rearrange("p (s r w) -> p s r w", s=3, w=NWIN)
                act(dst, src).then_inc(S["stat_copied"], 1)

            def row_stats(i, q, here):
                for t in range(TG):
                    for j in range(3):
                        slot, place = STAT_SLOT[t][j]
                        g = due(i, q, slot)
                        if g is not None and place == here:
                            stats(g, t, j)

            def gelu(g, e, hcs):
                for hc in hcs:
                    if hc == 0:
                        wait(eng, S["ffn2_done"], g * NE + e - 1)
                    eng.wait_ge(S["ffn1_done"], g * CHUNKS + NHC * e + hc + 1)
                    act(hid[:, e % 2, hc, :], bank[FFN1_BANK[(NHC * e + hc) % 3]][:, :], ACT.Gelu_apprx_tanh,
                        bias=b1s[:, e, hc:hc + 1]).then_inc(S["gelu_done"], 1)

            def scale_expert(g, par, e):
                eng.wait_ge(S["ffn2_done"], g * NE + e + 1)
                if e == 0:
                    eng.wait_ge(S["conf_ready"], g + 1)
                wait(eng, S["ffn_added"], g * NE + e)
                for t in range(TG):
                    last = act(scaled[:, t, :], bank[FFN2_BANK][:, t * CH:(t + 1) * CH],
                               scale=conf[:, par, t, e:e + 1])
                last.then_inc(S["expert_scaled"], 1)

            def chain(i, par, q, place):
                g = due(i, q, 37)
                if g is not None and place == "within":
                    eng.wait_ge(S["delta_ready"], g + 1)
                    act(th[:, :], delta[:, :], ACT.Tanh, scale=0.5).then_inc(S["tanh_ready"], 1)
                g = due(i, q, 39)
                if g is not None and place == "first":
                    eng.wait_ge(S["conf_transposed"], g + 1)
                    act(confT[:, :], C[0:TG * NE, 0:P]).then_inc(S["confT_ready"], 1)
                g = due(i, q, 21)
                if g is not None and place == "within":
                    eng.wait_ge(S["pooled_transposed"], g + 1)
                    act(h0[:, :, :].rearrange("p t c -> p (t c)"), A[:, :]).then_inc(S["h0_ready"], 1)
                g = due(i, q, 22)
                if g is not None and place == "first":
                    eng.wait_ge(S["norm_steps"], g * (2 * NORM) + NORM)
                    normalise(hn, h0, rstd, shift).then_inc(S["hn_ready"], 1)
                g = due(i, q, 23)
                if g is not None and place == "within":
                    eng.wait_ge(S["hn_transposed"], g + 1)
                    act(by_ch[:, :], C[:, :]).then_inc(S["hnT_ready"], 1)
                g = due(i, q, 24)
                if g is not None and place == "first":
                    for t in range(TG):
                        eng.wait_ge(S["projected"], g * 4 + t + 1)
                        act(xp[:, t, :, :].rearrange("p s c -> p (s c)"), bank[TOK_BANK[t % 3]][:, :])\
                            .then_inc(S["proj_copied"], 1)
                g = due(i, q, 34)
                if g is not None and place == "last":
                    eng.wait_ge(S["norm_steps"], g * (2 * NORM) + 2 * NORM)
                    normalise(xhat, h1[:, par], rstd, shift, 1).then_inc(S["xhat_ready"], 1)
                g = due(i, q, 35)
                if g is not None and place == "last":
                    eng.wait_ge(S["xhat_transposed"], g + 1)
                    wait(eng, S["ffn1_done"], g * CHUNKS - CHUNKS)
                    for dst, name in ((xn_hi[:, par, :], "xn_hi_ready"), (by_ch[:, :], "xnT_ready")):
                        act(dst, A[:, :], ACT.Identity, scale=ln_gc[:, :], bias=ln_bc[:, :])\
                            .then_inc(S[name], 1)
                    normalise(acc[:, par], h1[:, par], rstd, shift).then_inc(S["base_normed"], 1)
                g = due(i, q, 59)
                if g is not None and place == "last":
                    if at_step(g, 0):
                        eng.wait_ge(S["cls_out_steps"], CLS_OUT + 16)
                    wait(eng, S["out_stored"], g * (16 * IMG))
                    eng.wait_ge(S["out_norm_steps"], g * NORM + NORM)
                    normalise(ot, acc[:, 1 - par], rstdo, shifto).then_inc(S["out_normed"], 1)
                g = due(i, q, 62)
                if g is not None and place == "last":
                    eng.wait_ge(S["out_summed"], g + 1)
                    rows = out[bass.ds(g * (IMG * TG), IMG * TG), 1:T + 1, :].rearrange(
                        "(t m) s c -> m s t c", m=IMG)
                    for m in range(IMG):
                        eng.dma_start(rows[m], ot[m * T:(m + 1) * T, :, :]).then_inc(S["out_stored"], 16)

            def step(i, par):
                for q in range(NQ):
                    if at_step(i, 0):
                        cls_chain(q)
                    chain(i, par, q, "first")
                    for e in range(NE):
                        g = due(i, q, 37 + 2 * e)
                        if g is not None:
                            gelu(g, e, (0, 1))
                    for e in range(NE):
                        slot = 41 + 2 * e
                        g = due(i, q, slot)
                        if g is not None:
                            scale_expert(g, (par - slot // NQ) % 2, e)
                    chain(i, par, q, "within")
                    row_stats(i, q, "within")
                    for e in range(NE):
                        g = due(i, q, 37 + 2 * e)
                        if g is not None:
                            gelu(g, e, (2, 3))
                    row_stats(i, q, "last")
                    chain(i, par, q, "last")
                    for e in range(NE):
                        if at_slot(i, q, CLS_FFN + 2 * e):
                            cls_gelu(e)

            eng.wait_ge(S["pads_zeroed"], 3)
            schedule(step, eng.Fori)

        @block.vector
        def _(eng):
            V = nc.vector
            A, C, D = (bank[b] for b in TOK_BANK)

            def carry_wait():
                V.memset(wait_carrier[:, :], 0.0)

            def statistics(src, nt, s, base, bn6, mv):
                for t in range(nt):
                    last = V.bn_stats(bn6[:, t, :], src[:, t, :])
                last.then_inc(s, 1)
                eng.wait_ge(s, base + 1)
                carry_wait()
                for t in range(nt):
                    last = V.bn_aggr(mv[:, t, :], bn6[:, t, :])
                last.then_inc(s, 1)

            def normalise_cls(dst, src, mv, rstd, n=0):
                return V.tensor_scalar(dst[:, 0, :], src[:, 0, :], mv[:, 0, 0:1], rstd[:, n, 0:1],
                                       ALU.subtract, ALU.mult)

            def bc_tok(ap, nt):
                return ap.unsqueeze(1).to_broadcast([P, nt, CH])

            def top2(nt, src, s, v):
                V.tensor_copy(lg[:, 0:nt, :], src[:, 0:nt * NE].rearrange("p (t e) -> p t e", e=NE)).then_inc(s, 1)
                eng.wait_ge(s, v + 1)
                carry_wait()
                for t in range(nt):
                    last = V.max(top[:, t, :], lg[:, t, :])
                last.then_inc(s, 1)
                eng.wait_ge(s, v + 2)
                carry_wait()
                for t in range(nt):
                    last = V.max_index(top_i[:, t, :], top[:, t, :], lg[:, t, :])
                last.then_inc(s, 1)
                eng.wait_ge(s, v + 3)
                V.tensor_copy(top_f[:, 0:nt, 0:TOPK], top_i[:, 0:nt, 0:TOPK]).then_inc(s, 1)
                return V.tensor_tensor(delta[:, 0:nt], top[:, 0:nt, 0], top[:, 0:nt, 1], ALU.subtract)

            def confidences(conf, nt, s, v):
                V.tensor_scalar(c12[:, 0, 0:nt], th[:, 0:nt], 0.5, 0.5, ALU.mult, ALU.add)
                V.tensor_scalar(c12[:, 1, 0:nt], th[:, 0:nt], -0.5, 0.5, ALU.mult, ALU.add).then_inc(s, 1)
                for k in range(TOPK):
                    last = V.tensor_tensor(eq[:, k, 0:nt, :], iota[:, :].unsqueeze(1).to_broadcast([P, nt, NE]),
                                           top_f[:, 0:nt, k].unsqueeze(2).to_broadcast([P, nt, NE]), ALU.is_equal)
                last.then_inc(s, 1)
                eng.wait_ge(s, v + 2)
                for k in range(TOPK):
                    last = V.tensor_tensor(eq[:, k, 0:nt, :], eq[:, k, 0:nt, :],
                                           c12[:, k, 0:nt].unsqueeze(2).to_broadcast([P, nt, NE]), ALU.mult)
                last.then_inc(s, 1)
                eng.wait_ge(s, v + 3)
                return V.tensor_tensor(conf[:, 0:nt, :], eq[:, 0, 0:nt, :], eq[:, 1, 0:nt, :], ALU.add)

            def coefficients():
                n = [0]

                def link(ins):
                    n[0] += 1
                    ins.then_inc(S["coef_steps"], 1)
                    eng.wait_ge(S["coef_steps"], n[0])

                for src, dst in ((lambda k: cw[:, k, :], lambda k: coef_r[:, k, :]),
                                 (lambda k: coef_r[:, :, k], lambda k: coef[:, :, k])):
                    V.tensor_copy(dst(0), src(0))
                    V.tensor_copy(dst(4), src(2))
                    link(V.tensor_tensor(dst(1), src(0), src(1), ALU.add))
                    V.tensor_tensor(dst(3), src(1), src(2), ALU.add)
                    link(V.tensor_tensor(dst(2), dst(1), src(2), ALU.add))
                link(V.tensor_scalar(coef[:, :, :], coef[:, :, :], 1.0 / (POOL * POOL), None, ALU.mult))

            def cls_chain(q):
                s = S["cls_steps"]
                if q == 0:
                    eng.wait_ge(S["early_loaded"], N_EARLY)
                    V.memset(cls_conf[:, :, :], 0.0)
                    statistics(h0, 1, s, 0, bn6, mv)
                if q == 1:
                    eng.wait_ge(s, CLS["n5"])
                    normalise_cls(hn, h0, mv, rstd).then_inc(s, 1)
                if q == 2:
                    eng.wait_ge(s, CLS["spectra_sb"])
                    ft, f0 = bank[2], A
                    for k in range(STAGES):
                        cs = slice(k * CH, (k + 1) * CH)
                        V.tensor_tensor(cls_part[:, k, :], ft[:, cs], xp[:, 0, k, :], ALU.mult).then_inc(s, 1)
                        V.tensor_tensor(conv_sum[:, 0, :], f0[:, cs], xp[:, 0, k, :], ALU.mult).then_inc(s, 1)
                        eng.wait_ge(s, CLS[f"convolved{k}"])
                        V.tensor_tensor(xp[:, 0, k + 1, :], conv_sum[:, 0, :], xp[:, 0, k + 1, :], ALU.mult)\
                            .then_inc(s, 1)
                        eng.wait_ge(s, CLS[f"y{k}"])
                    V.tensor_tensor(cls_h1[:, 0, :], h0[:, 0, :], xp[:, 0, STAGES, :], ALU.add).then_inc(s, 1)
                    eng.wait_ge(s, CLS["h1"])
                    statistics(cls_h1, 1, s, CLS["h1"], bn6, mv)
                if q == 3:
                    eng.wait_ge(s, CLS["m5"])
                    for n, dst in enumerate((cls_acc, xhat)):
                        normalise_cls(dst, cls_h1, mv, rstd, n).then_inc(s, 1)
                if q == 4:
                    eng.wait_ge(s, CLS["xn_hi"])
                    V.tensor_tensor(xn_lo[:, 0:P], by_ch[:, 0:P], xn_hi[:, 0, 0:P].bitcast(F32), ALU.subtract)\
                        .then_inc(s, 1)
                if q == 5:
                    eng.wait_ge(s, CLS["logits"])
                    top2(1, C, s, CLS["logits"]).then_inc(s, 1)
                if q == 6:
                    eng.wait_ge(s, CLS["tanh"])
                    confidences(cls_conf, 1, s, CLS["tanh"]).then_inc(s, 1)
                if q == 7:
                    eng.wait_ge(s, CLS["bias"])
                    V.tensor_tensor(cls_acc[:, 0, :], D[:, 0:CH], cls_acc[:, 0, :], ALU.add).then_inc(s, 1)
                    coefficients()
                if q == 9:
                    eng.wait_ge(S["w1_split"], 1)
                    V.tensor_tensor(w1_lo[:, :, :], w1_stage, w1_hi[:, :, :].bitcast(F32), ALU.subtract)\
                        .then_inc(S["w1_split"], 1)

            def cls_add(e):
                eng.wait_ge(S["cls_ffn2"], e + 1)
                if e == 0:
                    eng.wait_ge(S["cls_steps"], CLS["base_b"])
                wait(eng, S["cls_added"], e)
                V.scalar_tensor_tensor(out=cls_acc[:, 0, :], in0=bank[CLS_BANK[e % 2]][:, 0:CH],
                                       scalar=cls_conf[:, 0, e:e + 1], in1=cls_acc[:, 0, :],
                                       op0=ALU.mult, op1=ALU.add).then_inc(S["cls_added"], 1)

            def row_sums(g, t, part):
                s, v, b = S["row_sums"], g * (3 * TG) + 3 * t, xb[:, t % 2]
                if part == 0:
                    eng.wait_ge(x_loaded[t % 2], (g * 2 + t // 2 + 1) * XLOAD)
                    V.tensor_tensor(b[:, 1:4, :], b[:, 1:4, :], b[:, 5:8, :], ALU.add).then_inc(s, 1)
                if part == 1:
                    for n, row in enumerate((1, 3)):
                        eng.wait_ge(s, v + 1 + n)
                        V.tensor_tensor(b[:, 2, :], b[:, 2, :], b[:, row, :], ALU.add).then_inc(s, 1)

            terms = [(2, 2), (3, 3)] + [(a, b) for a in range(5) for b in range(5) if (a, b) not in ((2, 2), (3, 3))]

            def convolve(g, half, lo, hi):
                s, v, size, img = S["conv_steps"], g * CONVS + half * HALF, GRID // 2, NWIN * W9
                for n in range(lo, hi):
                    a, b = terms[n]
                    (ra, di), (rb, dj) = TAPS[a], TAPS[b]
                    i0 = max(0, -di)
                    length = (NWIN - abs(di)) * W9 - max(0, dj)
                    o = PAD + half * size + (i0 + di) * W9 + dj
                    src = stat[:, 3 * ra + rb, o:o + size].rearrange("p (m f) -> p m f", f=img)[:, :, 0:length]
                    dst = pooled[:, n % 2, half * size:(half + 1) * size]\
                        .rearrange("p (m f) -> p m f", f=img)[:, :, i0 * W9:i0 * W9 + length]
                    if n == 0:
                        eng.wait_ge(S["stat_copied"], g * 12 + 6 * (half + 1))
                        wait(eng, s, v)
                        V.tensor_scalar(dst, src, coef[:, a, b:b + 1], cb[:, :], ALU.mult, ALU.add).then_inc(s, 1)
                    elif n == 1:
                        V.tensor_scalar(dst, src, coef[:, a, b:b + 1], None, ALU.mult).then_inc(s, 1)
                    else:
                        eng.wait_ge(s, v + n - 1)
                        V.scalar_tensor_tensor(out=dst, in0=src, scalar=coef[:, a, b:b + 1], in1=dst,
                                               op0=ALU.mult, op1=ALU.add).then_inc(s, 1)

            CONV_PLAN = ((11, 0, 0, 8), (13, 0, 8, 14), (14, 0, 14, 20), (15, 0, 20, 25),
                         (18, 1, 0, 12), (19, 1, 12, 21), (20, 1, 21, 25))

            def head(i, par, q):
                g = due(i, q, 21)
                if g is not None:
                    eng.wait_ge(S["conv_steps"], g * CONVS + 2 * HALF)
                    wait(eng, S["logits_ready"], g)
                    wait(eng, S["xn_lo_ready"], g)
                    a, b = (pooled[:, n, :].rearrange("p (r w) -> p r w", w=W9)[:, :, 0:NWIN] for n in range(2))
                    V.tensor_tensor(by_ch[:, :].rearrange("p (r w) -> p r w", w=NWIN), a, b, ALU.add)\
                        .then_inc(S["conv_steps"], 1)
                g = due(i, q, 37)
                if g is not None:
                    eng.wait_ge(S["logits_ready"], g + 1)
                    top2(TG, C, S["gate_steps"], g * 4).then_inc(S["delta_ready"], 1)
                g = due(i, q, 40)
                if g is not None:
                    eng.wait_ge(S["bias_ready"], g + 1)
                    eng.wait_ge(S["base_normed"], g + 1)
                    V.tensor_tensor(acc[:, par], D[:, :].rearrange("p (t c) -> p t c", c=CH), acc[:, par], ALU.add)\
                        .then_inc(S["base_ready"], 1)
                g = due(i, q, 57)
                if g is not None:
                    eng.wait_ge(S["ffn_added"], g * NE + NE)
                    wait(eng, S["out_normed"], g)
                    statistics(acc[:, 1 - par], TG, S["out_norm_steps"], g * NORM, bn6o, mvo)

            def tail(i, par, q):
                g = due(i, q, 21)
                if g is not None:
                    eng.wait_ge(S["h0_ready"], g + 1)
                    wait(eng, S["base_normed"], g)
                    statistics(h0, TG, S["norm_steps"], g * (2 * NORM), bn6, mv)
                g = due(i, q, 37)
                if g is not None:
                    eng.wait_ge(S["tanh_ready"], g + 1)
                    wait(eng, S["expert_scaled"], g * NE - NE)
                    confidences(conf[:, par], TG, S["mask_steps"], g * 3).then_inc(S["conf_ready"], 1)
                for k in range(STAGES):
                    g = due(i, q, 25 + 3 * k)
                    if g is not None:
                        for n, (z, f) in enumerate(((A, filt_re), (C, filt_im), (A, filt_im), (C, filt_re))):
                            if n < 2:
                                eng.wait_ge(S["spectrum_ready"], g * 6 + 2 * k + n + 1)
                            V.tensor_tensor(prod[:, n], z[:, :].rearrange("p (t c) -> p t c", c=CH),
                                            bc_tok(f[:, k, :], TG), ALU.mult).then_inc(S["product_ready"], 1)
                    g = due(i, q, 27 + 3 * k)
                    if g is not None:
                        eng.wait_ge(S["filtered"], g * 3 + k + 1)
                        V.tensor_tensor(conv_sum, D[:, :].rearrange("p (t c) -> p t c", c=CH),
                                        bc_tok(cls_part[:, k, :], TG), ALU.add).then_inc(S["conv_summed"], 1)
                        eng.wait_ge(S["conv_summed"], g * 3 + k + 1)
                        V.tensor_tensor(xp[:, :, k + 1, :], conv_sum, xp[:, :, k + 1, :], ALU.mult)\
                            .then_inc(S["y_ready"], 1)
                g = due(i, q, 33)
                if g is not None:
                    eng.wait_ge(S["y_ready"], g * 3 + 3)
                    wait(eng, S["out_summed"], g - 1)
                    V.tensor_tensor(h1[:, par], h0[:, :, :], xp[:, :, STAGES, :], ALU.add)\
                        .then_inc(S["h1_ready"], 1)
                    eng.wait_ge(S["h1_ready"], g + 1)
                    statistics(h1[:, par], TG, S["norm_steps"], g * (2 * NORM) + NORM, bn6, mv)

            def step(i, par):
                for q in range(NQ):
                    if at_step(i, 0):
                        cls_chain(q)
                    for e in range(NE):
                        if at_slot(i, q, CLS_FFN + 3 + 2 * e):
                            cls_add(e)
                    if at_slot(i, q, CLS_FFN + 2 + 2 * NE):
                        eng.wait_ge(S["cls_added"], NE)
                        statistics(cls_acc, 1, S["cls_out_steps"], 0, bn6o, mvo)
                    if at_slot(i, q, CLS_FFN + 4 + 2 * NE):
                        eng.wait_ge(S["cls_out_steps"], NORM)
                        normalise_cls(ot, cls_acc, mvo, rstdo).then_inc(S["cls_out_steps"], 1)
                    head(i, par, q)
                    tail_first = q == 21 % NQ
                    if tail_first:
                        tail(i, par, q)
                    for t in range(TG):
                        for part in range(2):
                            g = due(i, q, TILE_SLOT[t] + part)
                            if g is not None:
                                row_sums(g, t, part)
                    g = due(i, q, 36)
                    if g is not None:
                        eng.wait_ge(S["xnT_ready"], g + 1)
                        wait(eng, S["ffn1_done"], g * CHUNKS)
                        V.tensor_tensor(xn_lo[:, :], by_ch[:, :], xn_hi[:, par, :].bitcast(F32), ALU.subtract)\
                            .then_inc(S["xn_lo_ready"], 1)
                    for slot, half, lo, hi in CONV_PLAN:
                        g = due(i, q, slot)
                        if g is not None:
                            convolve(g, half, lo, hi)
                    if not tail_first:
                        tail(i, par, q)

            schedule(step, eng.Fori)


def kernel(x, cls_tok, L0_tok_conv_w, L0_tok_conv_b, L0_attn_W_proj, L0_attn_W_filt, L0_ffn_Wg, L0_ffn_W1,
           L0_ffn_b1, L0_ffn_W2, L0_ffn_b2, L0_ffn_ln_g, L0_ffn_ln_b, L0_ffn_out_g, L0_ffn_out_b):
    import concourse.bacc as bacc
    from concourse.bass_utils import run_bass_kernel_spmd

    a = np.asarray
    b2 = a(L0_ffn_b2)
    b2_blocks = np.zeros((TG, NE, TG, CH), b2.dtype)
    for t in range(TG):
        b2_blocks[t, :, t, :] = b2
    arrays = {
        "x": a(x),
        "cls_tok": a(cls_tok),
        "conv_w": a(L0_tok_conv_w).reshape(3, 3, CH).transpose(2, 0, 1),
        "conv_b": a(L0_tok_conv_b).reshape(CH, 1),
        "w_proj": a(L0_attn_W_proj).transpose(0, 2, 1).reshape(CH, -1),
        "w_filt": a(L0_attn_W_filt).transpose(0, 2, 1).reshape(CH, -1),
        "w_gate": a(L0_ffn_Wg),
        "w1": a(L0_ffn_W1).transpose(1, 0, 2),
        "b1": a(L0_ffn_b1).reshape(NE, NHC, P).transpose(2, 0, 1),
        "w2": a(L0_ffn_W2).reshape(NE, NHC, P, CH).transpose(2, 0, 1, 3),
        "b2_blocks": b2_blocks.reshape(TG * NE, TG, CH),
        "ln_g": a(L0_ffn_ln_g).reshape(CH, 1),
        "ln_b": a(L0_ffn_ln_b).reshape(CH, 1),
        "out_g": a(L0_ffn_out_g),
        "out_b": a(L0_ffn_out_b),
        **shape_constants(),
    }
    arrays = {f"in_{n}": np.ascontiguousarray(v) for n, v in arrays.items()}
    nc = bacc.Bacc("TRN2", target_bir_lowering=False, num_devices=1)
    args = [nc.dram_tensor(n, v.shape, mybir.dt.from_np(v.dtype), kind="ExternalInput").ap()
            for n, v in arrays.items()]
    out = nc.dram_tensor("out_dram", (B, T + 1, CH), F32, kind="ExternalOutput").ap()
    build(nc, *args, out)
    r = run_bass_kernel_spmd(nc, [arrays], core_ids=[0])
    return r.results[0]["out_dram"]
```
